# Optimizing a Trainium2 kernel written in Bass

```python
import numpy as np
import jax
import jax.numpy as jnp

def _softmax(x, axis=-1):
    return jax.nn.softmax(x, axis=axis)

def _gelu(x):
    return jax.nn.gelu(x, approximate=True)

def _silu(x):
    return jax.nn.silu(x)

def _sigmoid(x):
    return jax.nn.sigmoid(x)

def _layernorm(x, axis=-1, eps=1e-05):
    m = jnp.mean(x, axis=axis, keepdims=True)
    v = jnp.var(x, axis=axis, keepdims=True)
    return (x - m) / jnp.sqrt(v + eps)

def _scatter_add(tgt, idx, src, axis=0):
    return tgt.at[idx].add(src)

def _segment_sum(src, seg, n):
    return jax.ops.segment_sum(src, seg, n)
kernel_name = 'mk_xattn_ffn_d2_seqx_r8_4736c9'

def setup_inputs(seed: int=0):
    np.random.seed(seed)
    _w = jnp.asarray

    def _rec_inputs():
        import jax
        import jax.numpy as jnp
        _rk = jax.random.key(seed)
        x = -9.806e-05 + 1 * jax.random.normal(jax.random.fold_in(_rk, 1), (64, 128, 128), jnp.float32)
        _lenS = 128 - jax.random.randint(jax.random.fold_in(_rk, 7), (64,), 0, max(1, 128 // 4) + 1, jnp.int32)
        _lenS2 = 77 - jax.random.randint(jax.random.fold_in(_rk, 8), (64,), 0, max(1, 77 // 4) + 1, jnp.int32)
        _ctx_1024P = jax.random.normal(jax.random.fold_in(_rk, 11), (64, 16, 128), jnp.float32)
        _ctx_1024c = jax.random.dirichlet(jax.random.fold_in(_rk, 511), 0.3 * jnp.ones((16,), jnp.float32), (64, 77))
        _ctx_1024t = jnp.einsum('bsk,bkd->bsd', _ctx_1024c, _ctx_1024P)
        _ctx_1024t = _ctx_1024t * jax.lax.rsqrt(jnp.mean(jnp.square(_ctx_1024t)) + 1e-12) * 0.953939
        ctx_1024 = -1.52775e-05 + 0.999936 * (_ctx_1024t + 0.3 * jax.random.normal(jax.random.fold_in(_rk, 611), (64, 77, 128), jnp.float32))
        return (x, ctx_1024)
    x, ctx_1024 = _rec_inputs()

    def _L0_xattn_setup():
        import jax, jax.numpy as jnp
        import numpy as np
        D = 128
        NUM_ITERS = 3
        EPS = 1e-06
        SCALE = D ** (-0.5)

        def rmsnorm(x, w, eps=EPS):
            return x * jax.lax.rsqrt(jnp.mean(x * x, axis=-1, keepdims=True) + eps) * w

        def gru_cell(x, h, wih, whh, bih, bhh):
            gx = x @ wih.T + bih
            gh = h @ whh.T + bhh
            xr, xz, xn = jnp.split(gx, 3, axis=-1)
            hr, hz, hn = jnp.split(gh, 3, axis=-1)
            r = jax.nn.sigmoid(xr + hr)
            z = jax.nn.sigmoid(xz + hz)
            n = jnp.tanh(xn + r * hn)
            return (1.0 - z) * n + z * h
        key = jax.random.key(seed)
        ks = jax.random.split(key, 8)
        B, K, M, d = (8, 64, 512, D)
        w_std = d ** (-0.5)
        return {'slots': jax.random.normal(ks[0], (B, K, d), jnp.float32), 'P': jax.random.normal(ks[1], (B, M, d), jnp.float32), 'Wq': jax.random.normal(ks[2], (d, d), jnp.float32) * w_std, 'Wk': jax.random.normal(ks[3], (d, d), jnp.float32) * w_std, 'Wv': jax.random.normal(ks[4], (d, d), jnp.float32) * w_std, 'gru_wih': jax.random.normal(ks[5], (3 * d, d), jnp.float32) * w_std, 'gru_whh': jax.random.normal(ks[6], (3 * d, d), jnp.float32) * w_std, 'gru_bih': jnp.zeros((3 * d,), jnp.float32), 'gru_bhh': jnp.zeros((3 * d,), jnp.float32), 'slot_norm_w': jnp.ones((d,), jnp.float32), 'input_norm_w': jnp.ones((d,), jnp.float32)}
    _L0_xattn_all = _L0_xattn_setup()
    _L0_xattn_in = {k: v for k, v in _L0_xattn_all.items() if k in ('Wq', 'Wk', 'Wv', 'gru_wih', 'gru_whh', 'gru_bih', 'gru_bhh', 'slot_norm_w', 'input_norm_w')}
    del _L0_xattn_all

    def _L0_ffn_setup():
        import jax, jax.numpy as jnp
        import numpy as np
        TOP_K = 2
        EPS = 1e-06
        key = jax.random.key(seed)
        ks = jax.random.split(key, 6)
        B_, T, D = (8, 256, 128)
        E, R_ = (8, 16)
        scale = 1.0 / np.sqrt(D)
        x = jax.random.normal(ks[0], (B_, T, D), dtype=jnp.float32)
        W = jax.random.normal(ks[1], (D, D), dtype=jnp.float32) * scale
        b = jax.random.normal(ks[2], (D,), dtype=jnp.float32)
        R = jax.random.normal(ks[3], (E, D), dtype=jnp.float32) * scale
        A = jax.random.normal(ks[4], (E, R_, D), dtype=jnp.float32) * scale
        B = jax.random.normal(ks[5], (D, R_), dtype=jnp.float32)[None] * jnp.ones((E, 1, 1), jnp.float32)
        B = jax.random.normal(ks[5], (E, D, R_), dtype=jnp.float32) * (1.0 / np.sqrt(R_))
        return {'x': x, 'W': W, 'b': b, 'R': R, 'A': A, 'B': B}
    _L0_ffn_all = _L0_ffn_setup()
    _L0_ffn_in = {k: v for k, v in _L0_ffn_all.items() if k in ('W', 'b', 'R', 'A', 'B')}
    del _L0_ffn_all

    def _L1_xattn_setup():
        import jax, jax.numpy as jnp
        import numpy as np
        D_MODEL = 128
        NUM_HEADS = 16
        D_K = D_MODEL // NUM_HEADS
        key = jax.random.key(seed)
        ks = jax.random.split(key, 11)
        B, S, D = (4, 256, D_MODEL)
        scale = 1.0 / np.sqrt(D)
        return {'Q': jax.random.normal(ks[0], (B, S, D), jnp.float32), 'K': jax.random.normal(ks[1], (B, S, D), jnp.float32), 'V': jax.random.normal(ks[2], (B, S, D), jnp.float32), 'Wq': jax.random.normal(ks[3], (D, D), jnp.float32) * scale, 'bq': jnp.zeros((D,), jnp.float32), 'Wk': jax.random.normal(ks[4], (D, D), jnp.float32) * scale, 'bk': jnp.zeros((D,), jnp.float32), 'Wv': jax.random.normal(ks[5], (D, D), jnp.float32) * scale, 'bv': jnp.zeros((D,), jnp.float32), 'Wo': jax.random.normal(ks[6], (D, D), jnp.float32) * scale, 'bo': jnp.zeros((D,), jnp.float32)}
    _L1_xattn_all = _L1_xattn_setup()
    _L1_xattn_in = {k: v for k, v in _L1_xattn_all.items() if k in ('Wq', 'bq', 'Wk', 'bk', 'Wv', 'bv', 'Wo', 'bo')}
    del _L1_xattn_all

    def _L1_ffn_setup():
        import jax, jax.numpy as jnp
        import numpy as np
        import math
        N_EMBD = 128
        HIDDEN = 4 * N_EMBD
        N_EXPERTS = 8
        TOP_K = 2
        B, T = (4, 256)

        def new_gelu(x):
            c = math.sqrt(2.0 / math.pi)
            return 0.5 * x * (1.0 + jnp.tanh(c * (x + 0.044715 * x * x * x)))

        def _moe_forward(x, Wfc_s, bfc_s, Wproj_s, bproj_s, Wr, Wfc, bfc, Wproj, bproj):
            Bb, Tt, C = x.shape
            xf = x.reshape(Bb * Tt, C)
            N = Bb * Tt
            shared = new_gelu(xf @ Wfc_s + bfc_s) @ Wproj_s + bproj_s
            logits = xf @ Wr
            probs = jax.nn.softmax(logits, axis=-1)
            topk_p, topk_i = jax.lax.top_k(probs, TOP_K)
            topk_p = topk_p / jnp.sum(topk_p, axis=-1, keepdims=True)
            gate = jnp.zeros((N, N_EXPERTS), dtype=xf.dtype)
            gate = gate.at[jnp.arange(N)[:, None], topk_i].add(topk_p)
            routed = jnp.zeros_like(xf)
            for e in range(N_EXPERTS):
                h = new_gelu(xf @ Wfc[e] + bfc[e]) @ Wproj[e] + bproj[e]
                routed = routed + h * gate[:, e:e + 1]
            return (shared + routed).reshape(Bb, Tt, C)
        key = jax.random.key(seed)
        ks = jax.random.split(key, 10)
        s = 0.02
        return {'x': jax.random.normal(ks[0], (B, T, N_EMBD), dtype=jnp.float32), 'Wfc_s': jax.random.normal(ks[1], (N_EMBD, HIDDEN), dtype=jnp.float32) * s, 'bfc_s': jnp.zeros((HIDDEN,), dtype=jnp.float32), 'Wproj_s': jax.random.normal(ks[2], (HIDDEN, N_EMBD), dtype=jnp.float32) * s, 'bproj_s': jnp.zeros((N_EMBD,), dtype=jnp.float32), 'Wr': jax.random.normal(ks[3], (N_EMBD, N_EXPERTS), dtype=jnp.float32) * s, 'Wfc': jax.random.normal(ks[4], (N_EXPERTS, N_EMBD, HIDDEN), dtype=jnp.float32) * s, 'bfc': jnp.zeros((N_EXPERTS, HIDDEN), dtype=jnp.float32), 'Wproj': jax.random.normal(ks[5], (N_EXPERTS, HIDDEN, N_EMBD), dtype=jnp.float32) * s, 'bproj': jnp.zeros((N_EXPERTS, N_EMBD), dtype=jnp.float32)}
    _L1_ffn_all = _L1_ffn_setup()
    _L1_ffn_in = {k: v for k, v in _L1_ffn_all.items() if k in ('Wfc_s', 'bfc_s', 'Wproj_s', 'bproj_s', 'Wr', 'Wfc', 'bfc', 'Wproj', 'bproj')}
    del _L1_ffn_all
    return {'x': x, 'ctx_1024': ctx_1024, 'L0_xattn_Wq': _L0_xattn_in['Wq'], 'L0_xattn_Wk': _L0_xattn_in['Wk'], 'L0_xattn_Wv': _L0_xattn_in['Wv'], 'L0_xattn_gru_wih': _L0_xattn_in['gru_wih'], 'L0_xattn_gru_whh': _L0_xattn_in['gru_whh'], 'L0_xattn_gru_bih': _L0_xattn_in['gru_bih'], 'L0_xattn_gru_bhh': _L0_xattn_in['gru_bhh'], 'L0_xattn_slot_norm_w': _L0_xattn_in['slot_norm_w'], 'L0_xattn_input_norm_w': _L0_xattn_in['input_norm_w'], 'L0_ffn_W': _L0_ffn_in['W'], 'L0_ffn_b': _L0_ffn_in['b'], 'L0_ffn_R': _L0_ffn_in['R'], 'L0_ffn_A': _L0_ffn_in['A'], 'L0_ffn_B': _L0_ffn_in['B'], 'L1_xattn_Wq': _L1_xattn_in['Wq'], 'L1_xattn_bq': _L1_xattn_in['bq'], 'L1_xattn_Wk': _L1_xattn_in['Wk'], 'L1_xattn_bk': _L1_xattn_in['bk'], 'L1_xattn_Wv': _L1_xattn_in['Wv'], 'L1_xattn_bv': _L1_xattn_in['bv'], 'L1_xattn_Wo': _L1_xattn_in['Wo'], 'L1_xattn_bo': _L1_xattn_in['bo'], 'L1_ffn_Wfc_s': _L1_ffn_in['Wfc_s'], 'L1_ffn_bfc_s': _L1_ffn_in['bfc_s'], 'L1_ffn_Wproj_s': _L1_ffn_in['Wproj_s'], 'L1_ffn_bproj_s': _L1_ffn_in['bproj_s'], 'L1_ffn_Wr': _L1_ffn_in['Wr'], 'L1_ffn_Wfc': _L1_ffn_in['Wfc'], 'L1_ffn_bfc': _L1_ffn_in['bfc'], 'L1_ffn_Wproj': _L1_ffn_in['Wproj'], 'L1_ffn_bproj': _L1_ffn_in['bproj']}

def reference(x, ctx_1024, L0_xattn_Wq, L0_xattn_Wk, L0_xattn_Wv, L0_xattn_gru_wih, L0_xattn_gru_whh, L0_xattn_gru_bih, L0_xattn_gru_bhh, L0_xattn_slot_norm_w, L0_xattn_input_norm_w, L0_ffn_W, L0_ffn_b, L0_ffn_R, L0_ffn_A, L0_ffn_B, L1_xattn_Wq, L1_xattn_bq, L1_xattn_Wk, L1_xattn_bk, L1_xattn_Wv, L1_xattn_bv, L1_xattn_Wo, L1_xattn_bo, L1_ffn_Wfc_s, L1_ffn_bfc_s, L1_ffn_Wproj_s, L1_ffn_bproj_s, L1_ffn_Wr, L1_ffn_Wfc, L1_ffn_bfc, L1_ffn_Wproj, L1_ffn_bproj):
    import jax
    import jax.numpy as jnp

    def _L0_xattn_ref(slots, P, Wq, Wk, Wv, gru_wih, gru_whh, gru_bih, gru_bhh, slot_norm_w, input_norm_w):
        import jax, jax.numpy as jnp
        import numpy as np
        D = 128
        NUM_ITERS = 3
        EPS = 1e-06
        SCALE = D ** (-0.5)

        def rmsnorm(x, w, eps=EPS):
            return x * jax.lax.rsqrt(jnp.mean(x * x, axis=-1, keepdims=True) + eps) * w

        def gru_cell(x, h, wih, whh, bih, bhh):
            gx = x @ wih.T + bih
            gh = h @ whh.T + bhh
            xr, xz, xn = jnp.split(gx, 3, axis=-1)
            hr, hz, hn = jnp.split(gh, 3, axis=-1)
            r = jax.nn.sigmoid(xr + hr)
            z = jax.nn.sigmoid(xz + hz)
            n = jnp.tanh(xn + r * hn)
            return (1.0 - z) * n + z * h
        Pn = rmsnorm(P, input_norm_w)
        k_proj = Pn @ Wk.T
        v_proj = Pn @ Wv.T
        for _ in range(NUM_ITERS):
            sn = rmsnorm(slots, slot_norm_w)
            q_proj = sn @ Wq.T
            scores = jnp.einsum('bkd,bmd->bkm', q_proj, k_proj) * SCALE
            attn = jax.nn.softmax(scores, axis=-2)
            attn = attn / (jnp.sum(attn, axis=-1, keepdims=True) + EPS)
            updates = jnp.einsum('bkm,bmd->bkd', attn, v_proj)
            slots = gru_cell(updates, slots, gru_wih, gru_whh, gru_bih, gru_bhh)
        return slots

    def _L0_ffn_ref(x, W, b, R, A, B):
        import jax, jax.numpy as jnp
        import numpy as np
        TOP_K = 2
        EPS = 1e-06
        base_out = jnp.einsum('btd,od->bto', x, W) + b
        logits = jnp.einsum('btd,ed->bte', x, R)
        gate = jax.nn.softmax(logits, axis=-1)
        E = gate.shape[-1]
        _, idx = jax.lax.top_k(gate, TOP_K)
        mask = jax.nn.one_hot(idx, E, dtype=gate.dtype).sum(axis=-2)
        gate = gate * mask
        gate = gate / (gate.sum(axis=-1, keepdims=True) + EPS)
        h = jnp.einsum('btd,erd->bter', x, A)
        gh = gate[..., None] * h
        lora_out = jnp.einsum('bter,eor->bto', gh, B)
        return base_out + lora_out

    def _L1_xattn_ref(Q, K, V, Wq, bq, Wk, bk, Wv, bv, Wo, bo):
        import jax, jax.numpy as jnp
        import numpy as np
        D_MODEL = 128
        NUM_HEADS = 16
        D_K = D_MODEL // NUM_HEADS
        B, S, D = Q.shape
        H, Dk = (NUM_HEADS, D_K)

        def proj(x, W, b):
            y = jnp.einsum('bsd,de->bse', x, W.T) + b
            return y.reshape(B, -1, H, Dk).transpose(0, 2, 1, 3)
        q = proj(Q, Wq, bq)
        k = proj(K, Wk, bk)
        v = proj(V, Wv, bv)
        scores = jnp.einsum('bhqd,bhkd->bhqk', q, k) / np.sqrt(Dk)
        attn = jax.nn.softmax(scores, axis=-1)
        out = jnp.einsum('bhqk,bhkd->bhqd', attn, v)
        out = out.transpose(0, 2, 1, 3).reshape(B, -1, D)
        return jnp.einsum('bsd,de->bse', out, Wo.T) + bo

    def _L1_ffn_ref(x, Wfc_s, bfc_s, Wproj_s, bproj_s, Wr, Wfc, bfc, Wproj, bproj):
        import jax, jax.numpy as jnp
        import numpy as np
        import math
        N_EMBD = 128
        HIDDEN = 4 * N_EMBD
        N_EXPERTS = 8
        TOP_K = 2
        B, T = (4, 256)

        def new_gelu(x):
            c = math.sqrt(2.0 / math.pi)
            return 0.5 * x * (1.0 + jnp.tanh(c * (x + 0.044715 * x * x * x)))

        def _moe_forward(x, Wfc_s, bfc_s, Wproj_s, bproj_s, Wr, Wfc, bfc, Wproj, bproj):
            Bb, Tt, C = x.shape
            xf = x.reshape(Bb * Tt, C)
            N = Bb * Tt
            shared = new_gelu(xf @ Wfc_s + bfc_s) @ Wproj_s + bproj_s
            logits = xf @ Wr
            probs = jax.nn.softmax(logits, axis=-1)
            topk_p, topk_i = jax.lax.top_k(probs, TOP_K)
            topk_p = topk_p / jnp.sum(topk_p, axis=-1, keepdims=True)
            gate = jnp.zeros((N, N_EXPERTS), dtype=xf.dtype)
            gate = gate.at[jnp.arange(N)[:, None], topk_i].add(topk_p)
            routed = jnp.zeros_like(xf)
            for e in range(N_EXPERTS):
                h = new_gelu(xf @ Wfc[e] + bfc[e]) @ Wproj[e] + bproj[e]
                routed = routed + h * gate[:, e:e + 1]
            return (shared + routed).reshape(Bb, Tt, C)
        return _moe_forward(x, Wfc_s, bfc_s, Wproj_s, bproj_s, Wr, Wfc, bfc, Wproj, bproj)
    x = x + _L0_xattn_ref(_layernorm(x, axis=-1), ctx_1024, L0_xattn_Wq, L0_xattn_Wk, L0_xattn_Wv, L0_xattn_gru_wih, L0_xattn_gru_whh, L0_xattn_gru_bih, L0_xattn_gru_bhh, L0_xattn_slot_norm_w, L0_xattn_input_norm_w)
    x = x + _L0_ffn_ref(_layernorm(x, axis=-1), L0_ffn_W, L0_ffn_b, L0_ffn_R, L0_ffn_A, L0_ffn_B)
    x = x + _L1_xattn_ref(_layernorm(x, axis=-1), ctx_1024, ctx_1024, L1_xattn_Wq, L1_xattn_bq, L1_xattn_Wk, L1_xattn_bk, L1_xattn_Wv, L1_xattn_bv, L1_xattn_Wo, L1_xattn_bo)
    x = x + _L1_ffn_ref(_layernorm(x, axis=-1), L1_ffn_Wfc_s, L1_ffn_bfc_s, L1_ffn_Wproj_s, L1_ffn_bproj_s, L1_ffn_Wr, L1_ffn_Wfc, L1_ffn_bfc, L1_ffn_Wproj, L1_ffn_bproj)
    return x

_drawn_inputs = setup_inputs


def setup_inputs(seed=0):
    import zlib

    import numpy as np

    out = dict(_drawn_inputs(seed))
    spreads = {'L0_xattn_gru_bih': (0.0, 0.1),
     'L0_xattn_gru_bhh': (0.0, 0.1),
     'L0_xattn_slot_norm_w': (1.0, 0.2),
     'L0_xattn_input_norm_w': (1.0, 0.2),
     'L1_xattn_bq': (0.0, 0.67),
     'L1_xattn_bk': (0.0, 0.8),
     'L1_xattn_bv': (0.0, 0.1),
     'L1_xattn_bo': (0.0, 0.1),
     'L1_ffn_bfc_s': (0.0, 0.676),
     'L1_ffn_bproj_s': (0.0, 0.1),
     'L1_ffn_bfc': (0.0, 0.8),
     'L1_ffn_bproj': (0.0, 0.1)}
    factors = {'L1_ffn_Wfc': 3.187, 'L1_ffn_Wproj': 2.908}
    for name, (base, spread) in spreads.items():
        noise = np.random.default_rng([zlib.crc32(name.encode()), seed]).standard_normal(out[name].shape)
        drawn = base * np.exp(spread * noise) if base else spread * noise
        out[name] = jnp.asarray(drawn.astype(out[name].dtype))
    for name, factor in factors.items():
        out[name] = (out[name] * factor).astype(out[name].dtype)
    return out
```

```python
from contextlib import ExitStack

import numpy as np

import concourse.bass as bass
from concourse import mybir

F32 = mybir.dt.float32
I32 = mybir.dt.int32
ALU = mybir.AluOpType
ACT = mybir.ActivationFunctionType
AX_X = mybir.AxisListType.X

P = 128
GB = 4
GT = GB * P
CONSTS = 35
SLOTS_LINKS = 29
HEADS_LINKS = 47
TABLE_LINKS = 29
UNITS = 16
ER = 256
RMS_EPS = 1e-6
LN_EPS = 1e-5

STEPS = [
    ("heads", "norm"), ("slots", "turn"), ("heads", "project"), ("slots", "keys"),
    ("heads", "unit", 0), ("heads", "unit", 1),
    ("slots", "score", 0), ("heads", "unit", 2), ("heads", "unit", 3),
    ("slots", "share", 0), ("heads", "unit", 4),
    ("slots", "gates", 0), ("heads", "unit", 5), ("slots", "cell", 0), ("heads", "unit", 6),
    ("slots", "update", 0), ("heads", "unit", 7),
    ("slots", "score", 1), ("heads", "unit", 8), ("heads", "unit", 9),
    ("slots", "share", 1), ("heads", "unit", 10),
    ("slots", "gates", 1), ("heads", "unit", 11), ("slots", "cell", 1), ("heads", "unit", 12),
    ("slots", "update", 1), ("heads", "unit", 13),
    ("slots", "score", 2), ("heads", "unit", 14), ("heads", "unit", 15), ("heads", "unit", 16),
    ("slots", "share", 2), ("heads", "unit", 17),
    ("slots", "gates", 2), ("heads", "mix"), ("slots", "cell", 2), ("heads", "center"),
    ("slots", "update", 2), ("heads", "spread"),
    ("slots", "center"), ("heads", "route"), ("slots", "spread"), ("heads", "rank"),
    ("slots", "route"), ("slots", "turn_gate"), ("slots", "out"),
]


class Signals:
    def __init__(self, sem):
        self.table_chain = sem("table_chain")
        self.table_ready = sem("table_ready")
        self.pad_ready = sem("pad_ready")
        self.place_ready = sem("place_ready")
        self.pads_scattered = sem("pads_scattered")
        self.experts_in = sem("experts_in")
        self.shared_in = sem("shared_in")
        self.fc_s_done = sem("fc_s_done")
        self.y_now_ready = sem("y_now_ready")
        self.base_added = sem("base_added")
        self.waits_over = sem("waits_over")
        self.weights_in = sem("weights_in")
        self.columns_in = sem("columns_in")
        self.columns_turned = sem("columns_turned")
        self.consts_made = sem("consts_made")
        self.mask_made = sem("mask_made")
        self.turned_w = sem("turned_w")
        self.turned_w_out = sem("turned_w_out")
        self.fused_w = sem("fused_w")
        self.weights_ready = sem("weights_ready")
        self.x_in = sem("x_in")
        self.ctx_in = sem("ctx_in")
        self.ctx_squared = sem("ctx_squared")
        self.ctx_r_ready = sem("ctx_r_ready")
        self.ctx_ms_ready = sem("ctx_ms_ready")
        self.var_ready = sem("var_ready")
        self.stats_ready = sem("stats_ready")
        self.rs_ready = sem("rs_ready")
        self.slot_ln = sem("slot_ln")
        self.v1_ln = sem("v1_ln")
        self.v2_ln = sem("v2_ln")
        self.v3_ln = sem("v3_ln")
        self.rs1_ready = sem("rs1_ready")
        self.rs2_ready = sem("rs2_ready")
        self.rs3_ready = sem("rs3_ready")
        self.ctx_scale = sem("ctx_scale")
        self.xln_ready = sem("xln_ready")
        self.turned = sem("turned")
        self.slots_in = sem("slots_in")
        self.ctxT_ready = sem("ctxT_ready")
        self.xT_ready = sem("xT_ready")
        self.keys_done = sem("keys_done")
        self.keys_ready = sem("keys_ready")
        self.values_done = sem("values_done")
        self.values_by_act = sem("values_by_act")
        self.values_by_dve = sem("values_by_dve")
        self.squared = sem("squared")
        self.scored = sem("scored")
        self.sumsq_done = sem("sumsq_done")
        self.slot_r_ready = sem("slot_r_ready")
        self.score_read = sem("score_read")
        self.bias_ready = sem("bias_ready")
        self.exp_done = sem("exp_done")
        self.rz_ready = sem("rz_ready")
        self.share_summed = sem("share_summed")
        self.share_sum_read = sem("share_sum_read")
        self.share_ready = sem("share_ready")
        self.hn_done = sem("hn_done")
        self.r_done = sem("r_done")
        self.xn_done = sem("xn_done")
        self.z_done = sem("z_done")
        self.r_tanh_ready = sem("r_tanh_ready")
        self.z_tanh_ready = sem("z_tanh_ready")
        self.r_gate_ready = sem("r_gate_ready")
        self.cell_ready = sem("cell_ready")
        self.n_ready = sem("n_ready")
        self.s_less_n_ready = sem("s_less_n_ready")
        self.slots_new = sem("slots_new")
        self.x1_ready = sem("x1_ready")
        self.c1_done = sem("c1_done")
        self.c1_squared = sem("c1_squared")
        self.v1_done = sem("v1_done")
        self.xn1_ready = sem("xn1_ready")
        self.logits1_done = sem("logits1_done")
        self.down_done = sem("down_done")
        self.gate_shifted = sem("gate_shifted")
        self.gate_exp = sem("gate_exp")
        self.gate_ready = sem("gate_ready")
        self.gate_turned = sem("gate_turned")
        self.gate_T_ready = sem("gate_T_ready")
        self.down_ready = sem("down_ready")
        self.ffn1_done = sem("ffn1_done")
        self.x2_ready = sem("x2_ready")
        self.slots_chain = sem("slots_chain")
        self.c2_done = sem("c2_done")
        self.c2_squared = sem("c2_squared")
        self.v2_done = sem("v2_done")
        self.xn2_ready = sem("xn2_ready")
        self.q_done = sem("q_done")
        self.k_done = sem("k_done")
        self.v_done = sem("v_done")
        self.q_ready = sem("q_ready")
        self.q_masked = sem("q_masked")
        self.k_ready = sem("k_ready")
        self.v_ready = sem("v_ready")
        self.head_scored = sem("head_scored")
        self.head_shifted = sem("head_shifted")
        self.head_exp = sem("head_exp")
        self.head_turned = sem("head_turned")
        self.head_pT_ready = sem("head_pT_ready")
        self.head_summed = sem("head_summed")
        self.attended = sem("attended")
        self.wo_done = sem("wo_done")
        self.x3_ready = sem("x3_ready")
        self.c3_done = sem("c3_done")
        self.c3_squared = sem("c3_squared")
        self.v3_done = sem("v3_done")
        self.xn3_ready = sem("xn3_ready")
        self.logits2_done = sem("logits2_done")
        self.xn3_turned = sem("xn3_turned")
        self.xn3_tok_ready = sem("xn3_tok_ready")
        self.gap_ready = sem("gap_ready")
        self.gap_exp = sem("gap_exp")
        self.both_ready = sem("both_ready")
        self.ranks_done = sem("ranks_done")
        self.scatter_ready = sem("scatter_ready")
        self.heads_chain = sem("heads_chain")
        self.scattered = sem("scattered")
        self.x3_stored = sem("x3_stored")
        self.xn3_stored = sem("xn3_stored")


def two_layers(nc, x, ctx, wq0, wk0, wv0, wih, whh, bih, bhh, slot_w, in_w, w0, b0, r0, a0, lb0,
               wq1, bq1, wk1, bk1, wv1, bv1, wo1, bo1, wfc_s, bfc_s, wproj_s, bproj_s, wr, wfc, bfc,
               wproj, bproj, out):
    NB, S, D = x.shape
    M = ctx.shape[1]
    E = wr.shape[1]
    R = a0.shape[1]
    HID = wfc_s.shape[1]
    HC = HID // P
    NT = NB * S
    TILES = NT // P
    GROUPS = NB // GB
    NG = GROUPS
    CM = GB * M
    NH, DK = 16, D // 16
    Q = P // 32
    SCALE = float(D) ** -0.5
    HSCALE = float(DK) ** -0.5
    REGION = NT + ER
    EXPERT_TILES = (2 * NT + E * (ER - 1)) // ER
    assert S == P and D == P and E * R == P and NH == 4 * Q

    stack = ExitStack()
    with stack:
        def sb(name, shape, dt=F32):
            return stack.enter_context(nc.sbuf_tensor(name, shape, dt))

        def sem(name):
            return stack.enter_context(nc.semaphore(name))

        bank = [stack.enter_context(nc.psum_tensor(f"bank{i}", [P, 512], F32)) for i in range(8)]
        G0, G1, G2, G3, BS, BT, BO, BZ = bank

        x3_dram = nc.dram_tensor("x3_scratch", [P, NT], F32, kind="Internal").ap()
        xn3_dram = nc.dram_tensor("xn3_scratch", [P, NT], F32, kind="Internal").ap()
        rows_dram = nc.dram_tensor("expert_rows", [E * REGION, D], F32, kind="Internal").ap()
        y_dram = nc.dram_tensor("expert_out", [EXPERT_TILES * ER, D], F32, kind="Internal").ap()
        ends_dram = nc.dram_tensor("tile_table", [2, P], I32, kind="Internal").ap()

        NAT = sb("nat", [P, 17, P])
        TW = sb("turned_w", [P, 13, P])
        RT = sb("r0_turned", [P, E])
        WR = sb("wr", [P, E])
        KQ_W = sb("kq_w", [P, P])
        VG_W = sb("vg_w", [P, 3 * P])
        ident = sb("ident", [P, P])
        mean_w = sb("mean_w", [P, P])
        center_w = sb("center_w", [P, P])
        ones = sb("ones", [P, P])
        before = sb("before", [P, P])
        quad_mask = sb("quad_mask", [P, 4])
        quad_sel = sb("quad_sel", [P, 4, Q])
        first_w = sb("first_w", [P, E])
        region_at = sb("region_at", [P, E])
        first_i = sb("first_i", [P, E], I32)
        region_i = sb("region_i", [P, E], I32)
        sum_w = sb("sum_w", [P, 4, 32])
        vec_rows = sb("vec_rows", [13, P])
        col = sb("columns", [P, 13])
        IH, HH, SLOT_W, IN_W, B0, BQ, BK, BV, BO1 = 0, 3, 6, 7, 8, 9, 10, 11, 12
        half_b = sb("half_b", [P, 2])
        bo_all = sb("bo_all", [P, 1])
        WIH, WHH = TW[:, 0:3, :], TW[:, 3:6, :]
        W0_T, A0_T, LB_T, WQ_T, WK_T, WV_T, WO_T = (TW[:, i, :] for i in range(6, 13))

        scratch = sb("scratch", [P, 20 * GT])
        taken = [0]

        def share_a(partitions=P):
            taken[0] += GT
            return scratch[0:partitions, taken[0] - GT:taken[0]]

        x_tok = sb("x_tok", [P, GB, P])
        ctx_tok = sb("ctx_tok", [M, GB, P])
        stats = sb("stats", [P, GB, 6])
        mv = sb("mv", [P, GB, 2])
        var_tok = sb("var_tok", [P, GB])
        power = sb("power", [P, GB])
        rs_tok = sb("rs_tok", [P, GB])
        xln = sb("xln", [P, GB, P])
        ctx_sq = sb("ctx_sq", [M, GB, P])
        ctx_ms = sb("ctx_ms", [M, GB])
        ctx_r = sb("ctx_r", [M, GB])
        ctx_sc = sb("ctx_sc", [M, GB])
        ctx_nsc = sb("ctx_nsc", [M, GB])
        slots = sb("slots", [P, GT])
        xT = sb("xT", [P, GT])
        ctxT = sb("ctxT", [P, CM])
        keysT = sb("keysT", [P, CM])
        values = sb("values", [M, GB, 3 * P])
        slot_sq = share_a()
        slot_r = share_a(M)
        slot_ln = share_a(M)
        ln_buf = sb("ln_buf", [P, 2, GT])
        rms_eps = sb("rms_eps", [P, 1])
        ln_eps = sb("ln_eps", [P, 1])
        score = share_a(M)
        score_max = sb("score_max", [M, GB])
        score_b = sb("score_b", [M, GB])
        prob = sb("prob", [P, GT])
        prob_sum = sb("prob_sum", [M, GB])
        prob_rz = sb("prob_rz", [P, GB])
        share_rz = share_a(M)
        share = share_a(M)
        r_tanh = share_a()
        z_tanh = share_a()
        r_gate = share_a()
        hn_part = share_a()
        n_pre = share_a()
        n_new = share_a()
        s_less_n = share_a()
        z_part = share_a()
        x1 = sb("x1", [P, GT])
        c1_sq = share_a()
        rs1 = share_a()
        xn1 = share_a()
        top = {k: sb("top_" + k, [P, GB, E]) for k in ("pick", "one", "rest", "two", "both", "e", "low")}
        top1 = {k: sb("top1_" + k, [P, GB]) for k in ("m1", "b1", "m2", "b2", "z", "s", "g")}
        gate_x = sb("gate_x", [P, GB, E, R])
        gate_T = share_a()
        down = share_a()
        x2 = sb("x2", [P, GT])

        c2_sq = sb("c2_sq", [P, GT])
        rs2 = sb("rs2", [P, GT])
        xn2 = sb("xn2", [P, GT])
        q_all = share_a()
        q_mask = sb("q_mask", [P, 4, GT])
        k_quad = sb("k_quad", [P, GB, Q, M])
        v_pad = sb("v_pad", [M, GB * Q, 4 * (32 + DK)])
        head_max = sb("head_max", [P, 2, Q])
        head_s = sb("head_s", [P, 2, Q, M])
        head_p = sb("head_p", [P, 2, Q, M])
        head_pT = sb("head_pT", [M, 2, Q * P])
        o_rz = sb("o_rz", [P, GT])
        o_all = sb("o_all", [P, GT])
        x3 = sb("x3", [P, GT])
        c3_sq = sb("c3_sq", [P, GT])
        rs3 = sb("rs3", [P, GT])
        xn3 = sb("xn3", [P, GT])
        xn3_tok = sb("xn3_tok", [P, GB, P])
        mo = {k: sb("moe_" + k, [P, GB, E]) for k in ("pick", "one", "rest", "two", "both", "rank", "at", "t1", "t2")}
        mo1 = {k: sb("moe1_" + k, [P, GB]) for k in ("m1", "b1", "m2", "b2", "d", "e", "s", "row1", "row2")}
        count = sb("count", [P, E])
        scatter_at = sb("scatter_at", [P, 2, GB], I32)
        gate_of = sb("gate_of", [P, 2, TILES])
        rank_of = sb("rank_of", [P, 2, TILES])
        pick_of = sb("pick_of", [P, 2, TILES, E])

        zeros = sb("zeros", [P, P])
        lane_i = sb("lane_i", [P, 2], I32)
        lane = sb("lane", [P, 2])
        step_i = sb("step_i", [P, NT // ER], I32)
        step_at = sb("step_at", [P, NT // ER])
        tile_i = sb("tile_i", [P, EXPERT_TILES], I32)
        tile_no = sb("tile_no", [P, EXPERT_TILES])
        used = sb("used", [P, E, NT // ER])
        tiles_of = sb("tiles_of", [P, E])
        base_of = sb("base_of", [P, E + 1])
        past = sb("past", [P, EXPERT_TILES, E])
        past_w = sb("past_w", [P, EXPERT_TILES, E])
        tile_e = sb("tile_e", [P, EXPERT_TILES])
        tile_b = sb("tile_b", [P, EXPERT_TILES])
        tile_real = sb("tile_real", [P, EXPERT_TILES])
        tile_row = sb("tile_row", [P, EXPERT_TILES])
        table = sb("table", [P, 2, EXPERT_TILES], I32)
        pad_f = sb("pad_f", [P, 2, E])
        pad_at = sb("pad_at", [P, 2, E], I32)
        base_rows = sb("base_rows", [P, E])
        place_w = sb("place_w", [P, 2, TILES, E])
        place_f = sb("place_f", [P, 2, TILES])
        y_at = sb("y_at", [P, 2, TILES], I32)
        y_now = sb("y_now", [P, 2, 2, GB], I32)
        rows = sb("rows", [P, 2, 2, P])
        rowsT = sb("rowsT", [P, 2, ER])
        fc_w = sb("fc_w", [P, 2, HID])
        fc_b = sb("fc_b", [P, 2, HC])
        proj_w = sb("proj_w", [P, 2, HC * P])
        fc_all = scratch[:, 0:E * HID]
        proj_all = scratch[:, E * HID:2 * E * HID]
        fc_b_all = sb("fc_b_all", [P, E * HC])
        proj_b_all = sb("proj_b_all", [P, E, P])
        hidden = sb("hidden", [P, 2, HC, ER])
        y_out = sb("y_out", [P, 2, 2, P])
        fcs_w = sb("fcs_w", [P, HID])
        fcs_b = sb("fcs_b", [P, HC])
        projs_w = sb("projs_w", [P, HC, P])
        projs_b = sb("projs_b", [P, P])
        xn3_in = scratch[:, 0:2 * GT].rearrange("p (i n) -> p i n", i=2)
        x3_in = scratch[:, 2 * GT:4 * GT].rearrange("p (i n) -> p i n", i=2)
        hidden_s = scratch[:, 4 * GT:4 * GT + 2 * HC * GT].rearrange("p (i c n) -> p i c n", i=2, c=HC)
        y_in = scratch[:, 12 * GT:16 * GT].rearrange("p (i c b d) -> p i c b d", i=2, c=2, b=GB)
        gate_now = sb("gate_now", [P, 2, 2, GB])
        total = scratch[:, 16 * GT:18 * GT].rearrange("p (i b d) -> p i b d", i=2, b=GB)

        def pair(name):
            return [sem(f"{name}{i}") for i in range(2)]

        rows_in, rows_turned, rowsT_ready, fc_w_in, fc_done, gelu_done = map(
            pair, ("rows_in", "rows_turned", "rowsT_ready", "fc_w_in", "fc_done", "gelu_done"))
        proj_w_in, proj_done, y_ready, y_stored = map(pair, ("proj_w_in", "proj_done", "y_ready", "y_stored"))
        c_in, y_gathered, gelu_s_done, sum_done, total_ready, out_stored = map(
            pair, ("c_in", "y_gathered", "gelu_s_done", "sum_done", "total_ready", "out_stored"))

        s = Signals(sem)

        block = stack.enter_context(nc.Block())

        def loop(eng, first, end, body):
            body(first)
            if first + 1 < end:
                with eng.Fori(first + 1, end) as i:
                    body(i)

        def groups(eng, slots_step, heads_step):
            def take(step, t, a):
                if step[0] == "slots" and t is not None:
                    slots_step(t, *step[1:])
                if step[0] == "heads" and a is not None:
                    heads_step(a, *step[1:])

            for step in STEPS:
                take(step, 0, None)

            def both(t):
                for step in STEPS:
                    take(step, t, t - 1)

            loop(eng, 1, NG, both)
            for step in STEPS:
                take(step, None, NG - 1)

        FC = [(G0, G1), (G2, G3)]
        ROWS = [BS, BT]
        YP = [BO, BZ]
        EXPERT_LOADS = 16 * (2 * E + 2)
        PAIRS = EXPERT_TILES // 2
        assert EXPERT_TILES % 2 == 1 and NG % 2 == 0

        def wait_apart(eng, *waits):
            for signal, value in waits:
                eng.wait_ge(signal, value)
            eng.sem_inc(s.waits_over)

        class Chain:
            def __init__(self, eng, done, per):
                self.eng, self.done, self.per, self.n = eng, done, per, 0

            def start(self, t):
                self.base, self.n = t * self.per, 0

            def __call__(self, instruction):
                self.n += 1
                instruction.then_inc(self.done, 1)
                self.eng.wait_ge(self.done, self.base + self.n)

            def end(self):
                assert self.n == self.per, (self.done, self.n)

        @block.sync
        def _(sp):
            def load(dst, src):
                sp.dma_start(dst, src).then_inc(s.weights_in, 16)
            for i, w in enumerate((wk0, wq0, wv0)):
                load(NAT[:, i, :], w)
            load(NAT[:, 3:6, :], wih.rearrange("(k p) d -> p k d", p=P))
            load(NAT[:, 6:9, :], whh.rearrange("(k p) d -> p k d", p=P))
            load(NAT[:, 9, :], w0)
            load(NAT[:, 10, :], a0.rearrange("e r d -> (e r) d"))
            load(NAT[:, 11, :].rearrange("p (e r) -> p e r", e=E), lb0.rearrange("e o r -> o e r"))
            for i, w in enumerate((wq1, wk1, wv1, wo1)):
                load(NAT[:, 12 + i, :], w)
            load(NAT[0:E, 16, :], r0)
            load(WR[:, :], wr)

            def load_group(t):
                sp.wait_ge(s.turned, 3 * t)
                sp.dma_start(x_tok[:, :, :], x[bass.ds(t * GB, GB), :, :].rearrange("b s d -> s b d")
                             ).then_inc(s.x_in, 16)
                sp.wait_ge(s.ctx_squared, t)
                sp.dma_start(ctx_tok[:, :, :], ctx[bass.ds(t * GB, GB), :, :].rearrange("b s d -> s b d")
                             ).then_inc(s.ctx_in, 16)

            loop(sp, 0, NG, load_group)
            for e in range(E):
                sp.dma_start(proj_b_all[:, e, :], bproj[e:e + 1, :].broadcast_to([P, P])).then_inc(s.experts_in, 16)
                sp.dma_start(fc_b_all[:, e * HC:(e + 1) * HC], bfc[e, :].rearrange("(p c) -> p c", c=HC)
                             ).then_inc(s.experts_in, 16)
            for dst, src in ((fcs_w[:, :], wfc_s), (fcs_b[:, :], bfc_s.rearrange("(p c) -> p c", c=HC)),
                             (projs_w[:, :, :], wproj_s.rearrange("(p c) n -> p c n", c=HC)),
                             (projs_b[:, :], bproj_s.rearrange("(a n) -> a n", a=1).broadcast_to([P, P]))):
                sp.dma_start(dst, src).then_inc(s.shared_in, 16)

            sp.wait_ge(s.x2_ready, NG)
            sp.wait_ge(s.q_masked, 4 * NG)
            sp.dma_start(fc_all.rearrange("p (e h) -> p e h", e=E), wfc.rearrange("e d h -> d e h")
                         ).then_inc(s.experts_in, 16)
            sp.dma_start(proj_all.rearrange("p (e n) -> p e n", e=E), wproj.rearrange("e (p c) n -> p e (c n)", c=HC)
                         ).then_inc(s.experts_in, 16)

            def store_y(p, h, j):
                sp.wait_ge(y_ready[p], h + 1)
                sp.dma_start(y_dram[bass.ds(j * ER, ER), :].rearrange("(p c) d -> p c d", c=2), y_out[:, p, :, :]
                             ).then_inc(y_stored[p], 16)

            def tile_pair(m):
                for p in range(2):
                    store_y(p, m - 1, 2 * m - 2 + p)

            loop(sp, 1, PAIRS, tile_pair)
            store_y(0, PAIRS - 1, 2 * PAIRS - 2)
            store_y(1, PAIRS - 1, 2 * PAIRS - 1)
            store_y(0, PAIRS, 2 * PAIRS)

            sp.wait_ge(s.x3_stored, 16 * NG)
            sp.wait_ge(s.xn3_stored, 16 * NG)

            def load_c(p, h, g):
                sp.wait_ge(sum_done[p], h)
                cols = bass.ds(g * GT, GT)
                sp.dma_start(xn3_in[:, p, :], xn3_dram[:, cols]).then_inc(c_in[p], 16)
                sp.dma_start(x3_in[:, p, :], x3_dram[:, cols]).then_inc(c_in[p], 16)

            def store_out(p, h, g):
                sp.wait_ge(total_ready[p], h + 1)
                sp.dma_start(out[bass.ds(g * GB, GB), :, :].rearrange("b s d -> s b d"), total[:, p, :, :]
                             ).then_inc(out_stored[p], 16)

            load_c(0, 0, 0)
            load_c(1, 0, 1)
            def group_pair(m):
                for p in range(2):
                    load_c(p, m, 2 * m + p)
                    store_out(p, m - 1, 2 * m - 2 + p)

            loop(sp, 1, NG // 2, group_pair)
            for p in range(2):
                store_out(p, NG // 2 - 1, NG - 2 + p)
            for p in range(2):
                sp.wait_ge(out_stored[p], 16 * (NG // 2))

        @block.gpsimd
        def _(pool):
            made = [0]

            def make(instruction):
                made[0] += 1
                instruction.then_inc(s.consts_made, 1)

            def made_all():
                pool.wait_ge(s.consts_made, made[0])

            make(pool.memset(ident[:, :], 0.0))
            make(pool.memset(mean_w[:, :], 1.0 / D))
            make(pool.memset(ones[:, :], 1.0))
            make(pool.memset(quad_sel[:, :, :], 1.0))
            make(pool.memset(sum_w[:, :, :], 0.0))
            make(pool.memset(k_quad[:, :, :, :], 0.0))
            make(pool.memset(v_pad[:, :, :], 0.0))
            make(pool.memset(count[:, :], 0.0))
            make(pool.memset(power[:, :], -0.5))
            make(pool.memset(rms_eps[:, :], RMS_EPS))
            make(pool.memset(ln_eps[:, :], LN_EPS))
            make(pool.memset(prob[:, :], 0.0))
            make(pool.memset(prob_rz[:, :], 1.0))
            make(pool.memset(zeros[:, :], 0.0))
            make(pool.memset(base_of[:, :], 0.0))
            make(pool.iota(lane_i[:, :], [[P, 2]], base=0, channel_multiplier=1))
            make(pool.iota(step_i[:, :], [[ER, NT // ER]], base=0, channel_multiplier=0))
            make(pool.iota(tile_i[:, :], [[1, EXPERT_TILES]], base=0, channel_multiplier=0))
            make(pool.iota(first_i[:, :], [[-1, E]], base=E, channel_multiplier=0))
            make(pool.iota(region_i[:, :], [[1, E]], base=0, channel_multiplier=0))
            made_all()
            make(pool.affine_select(out=ident[:, :], in_=ident[:, :], compare_op=ALU.not_equal, fill=1.0,
                                    base=0, pattern=[[-1, P]], channel_multiplier=1))
            make(pool.affine_select(out=before[:, :], in_=ones[:, :], compare_op=ALU.is_gt, fill=0.0,
                                    base=0, pattern=[[1, P]], channel_multiplier=-1))
            make(pool.affine_select(out=quad_sel[:, :, :], in_=quad_sel[:, :, :], compare_op=ALU.is_ge, fill=0.0,
                                    base=0, pattern=[[-DK, 4], [-32, Q]], channel_multiplier=1))
            make(pool.affine_select(out=prob[:, :], in_=prob[:, :], compare_op=ALU.not_equal, fill=RMS_EPS,
                                    base=-M, pattern=[[0, GT]], channel_multiplier=1))
            for u in range(4):
                make(pool.memset(sum_w[:, u, DK * u:DK * u + DK], 1.0))
            make(pool.tensor_copy(first_w[:, :], first_i[:, :]))
            make(pool.tensor_copy(lane[:, :], lane_i[:, :]))
            make(pool.tensor_copy(step_at[:, :], step_i[:, :]))
            make(pool.tensor_copy(tile_no[:, :], tile_i[:, :]))
            made_all()
            make(pool.affine_select(out=quad_sel[:, :, :], in_=quad_sel[:, :, :], compare_op=ALU.is_ge, fill=0.0,
                                    base=DK - 1, pattern=[[DK, 4], [32, Q]], channel_multiplier=-1))
            make(pool.tensor_scalar(center_w[:, :], ident[:, :], 1.0 / D, None, ALU.subtract))
            make(pool.tensor_scalar(region_at[:, :], region_i[:, :], float(REGION), None, ALU.mult))
            assert made[0] == CONSTS
            for i, v in ((IH, bih), (HH, bhh)):
                pool.dma_start(vec_rows[i:i + 3, :], v.rearrange("(k p) -> k p", p=P)).then_inc(s.columns_in, 16)
            for i, v in ((SLOT_W, slot_w), (IN_W, in_w), (B0, b0), (BQ, bq1), (BK, bk1), (BV, bv1), (BO1, bo1)):
                pool.dma_start(vec_rows[i:i + 1, :], v.rearrange("(k p) -> k p", k=1)).then_inc(s.columns_in, 16)

            def slots_step(t, step, i=0):
                if step == "turn":
                    pool.wait_ge(s.ctx_in, 16 * t + 16)
                    pool.wait_ge(s.ctx_scale, t)
                    pool.tensor_tensor(ctx_sq[:, :, :], ctx_tok[:, :, :], ctx_tok[:, :, :], ALU.mult
                                       ).then_inc(s.ctx_squared, 1)
                    pool.wait_ge(s.var_ready, t + 1)
                    pool.tensor_tensor(rs_tok[:, :], var_tok[:, :], power[:, :], ALU.pow).then_inc(s.rs_ready, 1)
                    pool.wait_ge(s.ctx_ms_ready, t + 1)
                    pool.tensor_tensor(ctx_r[:, :], ctx_ms[:, :], power[0:M, :], ALU.pow).then_inc(s.ctx_r_ready, 1)
                if step == "score":
                    if i == 0:
                        pool.wait_ge(s.slots_in, t + 1)
                    else:
                        pool.wait_ge(s.slots_new, 3 * t + i)
                    pool.tensor_tensor(slot_sq[:, :], slots[:, :], slots[:, :], ALU.mult).then_inc(s.squared, 1)
                if step == "cell":
                    wait_apart(pool, (s.r_tanh_ready, 3 * t + i + 1))
                    pool.tensor_scalar(r_gate[:, :], r_tanh[:, :], 0.5, 0.5, ALU.mult, ALU.add
                                       ).then_inc(s.r_gate_ready, 1)
                if step == "update":
                    pool.wait_ge(s.n_ready, 3 * t + i + 1)
                    pool.tensor_tensor(s_less_n[:, :], slots[:, :], n_new[:, :], ALU.subtract
                                       ).then_inc(s.s_less_n_ready, 1)
                if step == "center":
                    pool.wait_ge(s.slots_new, 3 * t + 3)
                    pool.wait_ge(s.xT_ready, t + 1)
                    pool.tensor_tensor(x1[:, :], xT[:, :], slots[:, :], ALU.add).then_inc(s.x1_ready, 1)

            def heads_step(a, step, k=0):
                if step == "project":
                    pool.wait_ge(s.mask_made, 1)
                    pool.wait_ge(s.q_ready, a + 1)
                    for u in range(4):
                        pool.tensor_scalar(q_mask[:, u, :], q_all[:, :], quad_mask[:, u:u + 1], None, ALU.mult
                                           ).then_inc(s.q_masked, 1)
                if step == "center":
                    wait_apart(pool, (s.x3_ready, a + 1))
                    pool.dma_start(x3_dram[:, bass.ds(a * GT, GT)], x3[:, :]).then_inc(s.x3_stored, 16)
                if step == "rank":
                    wait_apart(pool, (s.xn3_ready, a + 1))
                    pool.dma_start(xn3_dram[:, bass.ds(a * GT, GT)], xn3[:, :]).then_inc(s.xn3_stored, 16)
                    wait_apart(pool, (s.xn3_tok_ready, a + 1), (s.scatter_ready, a + 1))
                    for c in range(2):
                        for b in range(GB):
                            pool.indirect_dma_start(
                                rows_dram, bass.IndirectOffsetOnAxis(ap=scatter_at[:, c, b:b + 1], axis=0),
                                xn3_tok[:, b, :], None).then_inc(s.scattered, 16)

            groups(pool, slots_step, heads_step)
            pool.wait_ge(s.pad_ready, 1)
            for c in range(2):
                for e in range(E):
                    pool.indirect_dma_start(rows_dram, bass.IndirectOffsetOnAxis(ap=pad_at[:, c, e:e + 1], axis=0),
                                            zeros[:, :], None).then_inc(s.pads_scattered, 16)
            pool.wait_ge(s.scattered, 128 * NG)
            pool.wait_ge(s.pads_scattered, 16 * 2 * E)
            pool.wait_ge(s.table_ready, 1)

            def load_rows(p, h, j):
                row = pool.value_load(table[0:1, 0, bass.ds(j, 1)], min_val=0, max_val=E * REGION - ER)
                wait_apart(pool, (rows_turned[p], h))
                pool.dma_start(rows[:, p, :, :], rows_dram[bass.ds(row, ER), :].rearrange("(p c) d -> p c d", c=2)
                               ).then_inc(rows_in[p], 16)

            def tile_pair(m):
                for p in range(2):
                    load_rows(p, m, 2 * m + p)

            loop(pool, 0, PAIRS, tile_pair)
            load_rows(0, PAIRS, 2 * PAIRS)

            pool.wait_ge(s.place_ready, 1)
            pool.wait_ge(y_stored[0], 16 * (PAIRS + 1))
            pool.wait_ge(y_stored[1], 16 * PAIRS)

            def gather(p, h, g):
                pool.wait_ge(total_ready[p], h)
                pool.tensor_copy(y_now[:, p, :, :], y_at[:, :, bass.ds(g * GB, GB)]).then_inc(s.y_now_ready, 1)
                wait_apart(pool, (s.y_now_ready, g + 1))
                for c in range(2):
                    for b in range(GB):
                        pool.indirect_dma_start(y_in[:, p, c, b, :], None, y_dram,
                                                bass.IndirectOffsetOnAxis(ap=y_now[:, p, c, b:b + 1], axis=0)
                                                ).then_inc(y_gathered[p], 16)

            def group_pair(m):
                for p in range(2):
                    gather(p, m, 2 * m + p)

            loop(pool, 0, NG // 2, group_pair)

        @block.scalar
        def _(act):
            def copy(dst, src, scale=1.0):
                return act.activation(dst, src, ACT.Copy, scale=scale)

            def inverse_root(ln, dst, src, eps, ln_signal, signal, n):
                act.activation(ln, src, ACT.Ln, bias=eps).then_inc(ln_signal, 1)
                act.wait_ge(ln_signal, n + 1)
                act.activation(dst, ln, ACT.Exp, scale=-0.5).then_inc(signal, 1)

            act.wait_ge(s.consts_made, CONSTS)
            act.wait_ge(s.turned_w, 4)
            copy(TW[:, 0:4, :], bank[0][:, :]).then_inc(s.turned_w_out, 1)
            copy(TW[:, 4:8, :], bank[1][:, :]).then_inc(s.turned_w_out, 1)

            def slots_step(t, step, i=0):
                n = 3 * t + i
                if step == "turn":
                    act.wait_ge(s.turned, 3 * t + 1)
                    copy(slots[:, :], G3[:, :]).then_inc(s.slots_in, 1)
                    act.wait_ge(s.turned, 3 * t + 3)
                    copy(xT[:, :], G2[:, :]).then_inc(s.xT_ready, 1)
                if step == "keys":
                    act.wait_ge(s.ctx_scale, t + 1)
                    for b, src in ((0, G0), (1, G2)):
                        act.wait_ge(s.values_done, 4 * t + b + 1)
                        copy(values[:, b, :], src[0:M, 0:3 * P], ctx_r[:, b:b + 1]).then_inc(s.values_by_act, 1)
                if step == "score":
                    act.wait_ge(s.sumsq_done, n + 1)
                    inverse_root(slot_ln[:, :], slot_r[:, :], G1[0:M, :], rms_eps[0:M, :], s.slot_ln, s.slot_r_ready, n)
                    act.wait_ge(s.bias_ready, n + 1)
                    for b in range(GB):
                        c = slice(b * P, (b + 1) * P)
                        last = act.activation(prob[0:M, c], score[:, c], ACT.Exp, bias=score_b[:, b:b + 1],
                                              scale=ctx_sc[:, b:b + 1], accum_out=prob_sum[:, b:b + 1])
                    last.then_inc(s.exp_done, 1)
                if step == "gates":
                    act.wait_ge(s.r_done, n + 1)
                    act.activation(r_tanh[:, :], G3[:, :], ACT.Tanh, bias=half_b[:, 0:1], scale=0.5
                                   ).then_inc(s.r_tanh_ready, 1)
                    act.wait_ge(s.z_done, n + 1)
                    act.activation(z_tanh[:, :], G1[:, :], ACT.Tanh, bias=half_b[:, 1:2], scale=0.5
                                   ).then_inc(s.z_tanh_ready, 1)
                if step == "cell":
                    act.wait_ge(s.cell_ready, n + 1)
                    act.activation(n_new[:, :], n_pre[:, :], ACT.Tanh, bias=col[:, IH + 2:IH + 3]
                                   ).then_inc(s.n_ready, 1)
                if step == "center":
                    act.wait_ge(s.c1_done, t + 1)
                    act.activation(c1_sq[:, :], G0[:, :], ACT.Square).then_inc(s.c1_squared, 1)
                if step == "spread":
                    act.wait_ge(s.v1_done, t + 1)
                    inverse_root(ln_buf[:, 0, :], rs1[:, :], G1[:, :], ln_eps[:, :], s.v1_ln, s.rs1_ready, t)
                if step == "route":
                    act.wait_ge(s.gate_shifted, t + 1)
                    act.activation(top["e"][:, :, :], top["low"][:, :, :], ACT.Exp).then_inc(s.gate_exp, 1)
                if step == "turn_gate":
                    act.wait_ge(s.gate_turned, t + 1)
                    copy(gate_T[:, :], G0[:, :]).then_inc(s.gate_T_ready, 1)

            def heads_step(a, step, k=0):
                n = UNITS * a + k
                if step == "norm":
                    act.wait_ge(s.c2_done, a + 1)
                    act.activation(c2_sq[:, :], BS[:, :], ACT.Square).then_inc(s.c2_squared, 1)
                    act.wait_ge(s.v2_done, a + 1)
                    inverse_root(ln_buf[:, 1, :], rs2[:, :], BT[:, :], ln_eps[:, :], s.v2_ln, s.rs2_ready, a)
                if step == "project":
                    act.wait_ge(s.q_done, a + 1)
                    act.activation(q_all[:, :], BS[:, :], ACT.Identity, bias=col[:, BQ:BQ + 1]
                                   ).then_inc(s.q_ready, 1)
                    act.wait_ge(s.v_done, a + 1)
                    copy(v_pad[:, :, :].rearrange("m c (u w) -> m c u w", u=4)[:, :, :, 0:DK],
                         BO[0:M, :].rearrange("m (c u d) -> m c u d", u=4, d=DK)).then_inc(s.v_ready, 1)
                if step == "unit":
                    if k < UNITS:
                        act.wait_ge(s.head_shifted, n + 1)
                        if k >= 2:
                            act.wait_ge(s.head_turned, n - 1)
                        else:
                            act.wait_ge(s.head_turned, UNITS * a)
                        act.activation(head_p[:, k % 2, :, :], head_s[:, k % 2, :, :], ACT.Exp, scale=HSCALE
                                       ).then_inc(s.head_exp, 1)
                    if 1 <= k <= UNITS:
                        j = k - 1
                        act.wait_ge(s.head_turned, UNITS * a + j + 1)
                        if j >= 2:
                            act.wait_ge(s.head_summed, UNITS * a + j - 1)
                        else:
                            act.wait_ge(s.head_summed, UNITS * a)
                        copy(head_pT[:, j % 2, :], BT[0:M, :]).then_inc(s.head_pT_ready, 1)
                if step == "center":
                    act.wait_ge(s.c3_done, a + 1)
                    act.activation(c3_sq[:, :], BT[:, :], ACT.Square).then_inc(s.c3_squared, 1)
                if step == "spread":
                    act.wait_ge(s.v3_done, a + 1)
                    inverse_root(ln_buf[:, 1, :], rs3[:, :], BZ[:, :], ln_eps[:, :], s.v3_ln, s.rs3_ready, a)
                if step == "route":
                    act.wait_ge(s.xn3_turned, a + 1)
                    act.wait_ge(s.scattered, 128 * a)
                    copy(xn3_tok[:, :, :], BT[:, :]).then_inc(s.xn3_tok_ready, 1)
                    act.wait_ge(s.gap_ready, a + 1)
                    act.activation(mo1["e"][:, :], mo1["d"][:, :], ACT.Exp).then_inc(s.gap_exp, 1)

            groups(act, slots_step, heads_step)

            act.wait_ge(s.table_ready, 1)
            act.wait_ge(s.experts_in, EXPERT_LOADS)

            def take_proj_w(p, h, j):
                e = act.value_load(table[0:1, 1, bass.ds(j, 1)], min_val=0, max_val=E - 1)
                act.wait_ge(proj_done[p], h)
                act.activation(proj_w[:, p, :], proj_all[:, bass.ds(e * (HC * P), HC * P)], ACT.Copy
                               ).then_inc(proj_w_in[p], 1)

            def gelu(p, h):
                act.wait_ge(fc_w_in[p], h + 1)
                act.wait_ge(proj_done[p], h)
                act.wait_ge(fc_done[p], h + 1)
                for c in range(HC):
                    last = act.activation(hidden[:, p, c, :], FC[p][c // 2][:, (c % 2) * ER:(c % 2 + 1) * ER],
                                          ACT.Gelu_apprx_tanh, bias=fc_b[:, p, c:c + 1])
                last.then_inc(gelu_done[p], 1)

            def tile_pair(m):
                for p in range(2):
                    take_proj_w(p, m, 2 * m + p)
                    gelu(p, m)

            loop(act, 0, PAIRS, tile_pair)
            take_proj_w(0, PAIRS, 2 * PAIRS)
            gelu(0, PAIRS)

            act.wait_ge(s.shared_in, 64)

            def gelu_shared(p, h, g):
                act.wait_ge(sum_done[p], h)
                for c in range(HC):
                    act.wait_ge(s.fc_s_done, HC * g + c + 1)
                    act.activation(hidden_s[:, p, c, :], bank[c][:, :], ACT.Gelu_apprx_tanh, bias=fcs_b[:, c:c + 1]
                                   ).then_inc(gelu_s_done[p], 1)

            def group_pair(m):
                for p in range(2):
                    gelu_shared(p, m, 2 * m + p)

            loop(act, 0, NG // 2, group_pair)

        @block.vector
        def _(dve):
            dve.wait_ge(s.consts_made, CONSTS)
            dve.reduce_sum(quad_mask[:, :], quad_sel[:, :, :], AX_X).then_inc(s.mask_made, 1)
            setup = Chain(dve, s.weights_ready, 9)
            setup.start(0)
            dve.wait_ge(s.columns_turned, 1)
            setup(dve.tensor_copy(col[:, :], bank[7][:, 0:13]))
            setup(dve.tensor_tensor(half_b[:, :], col[:, IH:IH + 2], col[:, HH:HH + 2], ALU.add))
            setup(dve.tensor_scalar(half_b[:, :], half_b[:, :], 0.5, None, ALU.mult))
            dve.wait_ge(s.turned_w, 4)
            setup(dve.tensor_copy(TW[:, 8:12, :], bank[2][:, :]))
            setup(dve.tensor_copy(TW[:, 12, :], bank[3][:, 0:P]))
            setup(dve.tensor_copy(RT[:, :], bank[3][:, P:P + E]))
            dve.wait_ge(s.fused_w, 3)
            setup(dve.tensor_scalar(KQ_W[:, :], bank[4][:, 0:P], col[:, IN_W:IN_W + 1], None, ALU.mult))
            setup(dve.tensor_scalar(VG_W[:, :], bank[5][:, 0:3 * P], col[:, IN_W:IN_W + 1], None, ALU.mult))
            setup(dve.tensor_tensor(bo_all[:, :], bank[6][:, 0:1], col[:, BO1:BO1 + 1], ALU.add))
            setup.end()

            slots_link = Chain(dve, s.slots_chain, SLOTS_LINKS)
            heads_link = Chain(dve, s.heads_chain, HEADS_LINKS)

            def first_two(link, src, w, w1):
                m1, b1, m2, b2 = (w1[k][:, :] for k in ("m1", "b1", "m2", "b2"))
                order = first_w[:, :].unsqueeze(1).broadcast_to([P, GB, E])
                spread = lambda v: v.unsqueeze(2).broadcast_to([P, GB, E])
                link(dve.reduce_max(m1, src, AX_X))
                link(dve.tensor_tensor(w["pick"][:, :, :], src, spread(m1), ALU.is_equal))
                link(dve.tensor_tensor(w["pick"][:, :, :], w["pick"][:, :, :], order, ALU.mult))
                link(dve.reduce_max(b1, w["pick"][:, :, :], AX_X))
                link(dve.tensor_tensor(w["one"][:, :, :], w["pick"][:, :, :], spread(b1), ALU.is_equal))
                link(dve.scalar_tensor_tensor(w["rest"][:, :, :], w["one"][:, :, :], -3.0e38, src, ALU.mult, ALU.add))
                link(dve.reduce_max(m2, w["rest"][:, :, :], AX_X))
                link(dve.tensor_tensor(w["pick"][:, :, :], w["rest"][:, :, :], spread(m2), ALU.is_equal))
                link(dve.tensor_tensor(w["pick"][:, :, :], w["pick"][:, :, :], order, ALU.mult))
                link(dve.reduce_max(b2, w["pick"][:, :, :], AX_X))
                link(dve.tensor_tensor(w["two"][:, :, :], w["pick"][:, :, :], spread(b2), ALU.is_equal))

            def slots_step(t, step, i=0):
                link = slots_link
                n = 3 * t + i
                if step == "turn":
                    link.start(t)
                    dve.wait_ge(s.x_in, 16 * t + 16)
                    for b in range(GB):
                        last = dve.bn_stats(stats[:, b, :], x_tok[:, b, :])
                    last.then_inc(s.stats_ready, 1)
                    wait_apart(dve, (s.stats_ready, t + 1))
                    for b in range(GB):
                        last = dve.bn_aggr(mv[:, b, :], stats[:, b, :])
                    link(last)
                    dve.tensor_scalar(var_tok[:, :], mv[:, :, 1], LN_EPS, None, ALU.add).then_inc(s.var_ready, 1)
                    dve.wait_ge(s.rs_ready, t + 1)
                    for b in range(GB):
                        last = dve.tensor_scalar(xln[:, b, :], x_tok[:, b, :], mv[:, b, 0:1], rs_tok[:, b:b + 1],
                                                 ALU.subtract, ALU.mult)
                    last.then_inc(s.xln_ready, 1)
                    dve.wait_ge(s.ctx_squared, t + 1)
                    link(dve.reduce_sum(ctx_ms[:, :], ctx_sq[:, :, :], AX_X))
                    dve.tensor_scalar(ctx_ms[:, :], ctx_ms[:, :], 1.0 / D, RMS_EPS, ALU.mult, ALU.add
                                      ).then_inc(s.ctx_ms_ready, 1)
                    dve.wait_ge(s.ctx_r_ready, t + 1)
                    dve.tensor_scalar(ctx_sc[:, :], ctx_r[:, :], SCALE, None, ALU.mult)
                    dve.tensor_scalar(ctx_nsc[:, :], ctx_r[:, :], -SCALE, None, ALU.mult).then_inc(s.ctx_scale, 1)
                    dve.wait_ge(s.turned, 3 * t + 2)
                    dve.wait_ge(s.k_done, t)
                    dve.tensor_copy(ctxT[:, :], G0[:, 0:CM]).then_inc(s.ctxT_ready, 1)
                if step == "keys":
                    dve.wait_ge(s.keys_done, t + 1)
                    dve.tensor_scalar(keysT[:, :], G1[:, 0:CM], col[:, SLOT_W:SLOT_W + 1], None, ALU.mult
                                      ).then_inc(s.keys_ready, 1)
                    dve.wait_ge(s.ctx_scale, t + 1)
                    for b, src in ((2, G3), (3, G1)):
                        dve.wait_ge(s.values_done, 4 * t + b + 1)
                        dve.tensor_scalar(values[:, b, :], src[0:M, 0:3 * P], ctx_r[:, b:b + 1], None, ALU.mult
                                          ).then_inc(s.values_by_dve, 1)
                if step == "score":
                    dve.wait_ge(s.slot_r_ready, n + 1)
                    dve.wait_ge(s.scored, n + 1)
                    dve.tensor_tensor(score[:, :], G0[0:M, :], slot_r[:, :], ALU.mult).then_inc(s.score_read, 1)
                    dve.wait_ge(s.score_read, n + 1)
                    link(dve.reduce_max(score_max[:, :], score[:, :].rearrange("m (b k) -> m b k", b=GB), AX_X))
                    dve.tensor_tensor(score_b[:, :], score_max[:, :], ctx_nsc[:, :], ALU.mult
                                      ).then_inc(s.bias_ready, 1)
                if step == "share":
                    dve.wait_ge(s.exp_done, n + 1)
                    dve.reciprocal(prob_rz[0:M, :], prob_sum[:, :]).then_inc(s.rz_ready, 1)
                    dve.wait_ge(s.share_summed, n + 1)
                    dve.reciprocal(share_rz[:, :], G2[0:M, :]).then_inc(s.share_sum_read, 1)
                    dve.wait_ge(s.share_sum_read, n + 1)
                    for b in range(GB):
                        c = slice(b * P, (b + 1) * P)
                        last = dve.scalar_tensor_tensor(share[:, c], prob[0:M, c], prob_rz[0:M, b:b + 1],
                                                        share_rz[:, c], ALU.mult, ALU.mult)
                    last.then_inc(s.share_ready, 1)
                if step == "cell":
                    dve.wait_ge(s.hn_done, n + 1)
                    dve.wait_ge(s.r_gate_ready, n + 1)
                    link(dve.scalar_tensor_tensor(hn_part[:, :], G2[:, :], col[:, HH + 2:HH + 3], r_gate[:, :],
                                                  ALU.add, ALU.mult))
                    dve.wait_ge(s.xn_done, n + 1)
                    dve.tensor_tensor(n_pre[:, :], G0[:, :], hn_part[:, :], ALU.add).then_inc(s.cell_ready, 1)
                if step == "update":
                    dve.wait_ge(s.z_tanh_ready, n + 1)
                    dve.wait_ge(s.s_less_n_ready, n + 1)
                    link(dve.scalar_tensor_tensor(z_part[:, :], z_tanh[:, :], 1.0, s_less_n[:, :], ALU.add, ALU.mult))
                    dve.scalar_tensor_tensor(slots[:, :], z_part[:, :], 0.5, n_new[:, :], ALU.mult, ALU.add
                                             ).then_inc(s.slots_new, 1)
                if step == "spread":
                    dve.wait_ge(s.rs1_ready, t + 1)
                    dve.tensor_tensor(xn1[:, :], G0[:, :], rs1[:, :], ALU.mult).then_inc(s.xn1_ready, 1)
                if step == "route":
                    dve.wait_ge(s.logits1_done, t + 1)
                    logits = G2[:, 0:GB * E].rearrange("p (b e) -> p b e", b=GB)
                    spread = lambda v: v.unsqueeze(2).broadcast_to([P, GB, E])
                    first_two(link, logits, top, top1)
                    dve.tensor_tensor(top["low"][:, :, :], logits, spread(top1["m1"][:, :]), ALU.subtract
                                      ).then_inc(s.gate_shifted, 1)
                    link(dve.tensor_tensor(top["both"][:, :, :], top["one"][:, :, :], top["two"][:, :, :], ALU.add))
                    dve.wait_ge(s.gate_exp, t + 1)
                    link(dve.reduce_sum(top1["z"][:, :], top["e"][:, :, :], AX_X))
                    link(dve.tensor_tensor(top["both"][:, :, :], top["both"][:, :, :], top["e"][:, :, :], ALU.mult))
                    link(dve.reduce_sum(top1["s"][:, :], top["both"][:, :, :], AX_X))
                    link(dve.scalar_tensor_tensor(top1["g"][:, :], top1["z"][:, :], RMS_EPS, top1["s"][:, :],
                                                  ALU.mult, ALU.add))
                    link(dve.reciprocal(top1["g"][:, :], top1["g"][:, :]))
                    link(dve.tensor_tensor(top["both"][:, :, :], top["both"][:, :, :], spread(top1["g"][:, :]),
                                           ALU.mult))
                    dve.tensor_copy(gate_x[:, :, :, :],
                                    top["both"][:, :, :].unsqueeze(3).broadcast_to([P, GB, E, R])
                                    ).then_inc(s.gate_ready, 1)
                if step == "turn_gate":
                    dve.wait_ge(s.gate_T_ready, t + 1)
                    dve.wait_ge(s.down_done, t + 1)
                    dve.tensor_tensor(down[:, :], G3[:, :], gate_T[:, :], ALU.mult).then_inc(s.down_ready, 1)
                if step == "out":
                    dve.wait_ge(s.ffn1_done, t + 1)
                    dve.scalar_tensor_tensor(x2[:, :], G1[:, :], col[:, B0:B0 + 1], x1[:, :], ALU.add, ALU.add
                                             ).then_inc(s.x2_ready, 1)
                    link.end()

            def heads_step(a, step, k=0):
                link = heads_link
                n = UNITS * a + k
                if step == "norm":
                    link.start(a)
                    dve.wait_ge(s.rs2_ready, a + 1)
                    dve.tensor_tensor(xn2[:, :], BS[:, :], rs2[:, :], ALU.mult).then_inc(s.xn2_ready, 1)
                if step == "project":
                    dve.wait_ge(s.k_done, a + 1)
                    for g in range(Q):
                        rows = slice(32 * g, 32 * g + 32)
                        last = dve.tensor_scalar(k_quad[rows, :, g, :],
                                                 BT[rows, 0:CM].rearrange("p (b m) -> p b m", b=GB),
                                                 col[rows, BK:BK + 1], None, ALU.add)
                    last.then_inc(s.k_ready, 1)
                if step == "unit" and k < UNITS:
                    dve.wait_ge(s.head_scored, n + 1)
                    sc = BS[:, 0:Q * M].rearrange("p (g m) -> p g m", g=Q)
                    link(dve.reduce_max(head_max[:, k % 2, :], sc, AX_X))
                    if k >= 2:
                        dve.wait_ge(s.head_exp, n - 1)
                    else:
                        dve.wait_ge(s.head_exp, UNITS * a)
                    dve.tensor_tensor(head_s[:, k % 2, :, :], sc,
                                      head_max[:, k % 2, :].unsqueeze(2).broadcast_to([P, Q, M]), ALU.subtract
                                      ).then_inc(s.head_shifted, 1)
                if step == "mix":
                    dve.wait_ge(s.head_summed, UNITS * (a + 1))
                    link(dve.reciprocal(o_rz[:, :], BZ[:, :]))
                    dve.tensor_tensor(o_all[:, :], BO[:, :], o_rz[:, :], ALU.mult).then_inc(s.attended, 1)
                    dve.wait_ge(s.wo_done, a + 1)
                    dve.wait_ge(s.x3_stored, 16 * a)
                    dve.scalar_tensor_tensor(x3[:, :], BS[:, :], bo_all[:, 0:1], x2[:, :], ALU.add, ALU.add
                                             ).then_inc(s.x3_ready, 1)
                if step == "spread":
                    dve.wait_ge(s.rs3_ready, a + 1)
                    dve.wait_ge(s.xn3_stored, 16 * a)
                    dve.tensor_tensor(xn3[:, :], BT[:, :], rs3[:, :], ALU.mult).then_inc(s.xn3_ready, 1)
                if step == "route":
                    dve.wait_ge(s.logits2_done, a + 1)
                    logits = BO[:, 0:GB * E].rearrange("p (b e) -> p b e", b=GB)
                    first_two(link, logits, mo, mo1)
                    dve.tensor_tensor(mo["both"][:, :, :], mo["one"][:, :, :], mo["two"][:, :, :], ALU.add
                                      ).then_inc(s.both_ready, 1)
                    dve.tensor_tensor(mo1["d"][:, :], mo1["m2"][:, :], mo1["m1"][:, :], ALU.subtract
                                      ).then_inc(s.gap_ready, 1)
                    tiles = bass.ds(a * GB, GB)
                    dve.tensor_copy(pick_of[:, 0, tiles, :], mo["one"][:, :, :])
                    dve.tensor_copy(pick_of[:, 1, tiles, :], mo["two"][:, :, :])
                if step == "rank":
                    tiles = bass.ds(a * GB, GB)
                    dve.wait_ge(s.gap_exp, a + 1)
                    link(dve.tensor_scalar(mo1["s"][:, :], mo1["e"][:, :], 1.0, None, ALU.add))
                    link(dve.reciprocal(mo1["s"][:, :], mo1["s"][:, :]))
                    dve.tensor_copy(gate_of[:, 0, tiles], mo1["s"][:, :])
                    dve.tensor_tensor(gate_of[:, 1, tiles], mo1["s"][:, :], mo1["e"][:, :], ALU.mult)
                    dve.wait_ge(s.ranks_done, a + 1)
                    for b in range(GB):
                        dve.tensor_tensor(mo["rank"][:, b, :], BS[:, b * E:(b + 1) * E], count[:, :], ALU.add)
                        link(dve.tensor_tensor(count[:, :], BS[:, (GB + b) * E:(GB + b + 1) * E], count[:, :], ALU.add))
                    link(dve.tensor_tensor(mo["at"][:, :, :], mo["rank"][:, :, :],
                                           region_at[:, :].unsqueeze(1).broadcast_to([P, GB, E]), ALU.add))
                    dve.wait_ge(s.scattered, 128 * a)
                    for c, pick in enumerate(("one", "two")):
                        link(dve.tensor_tensor(mo["t1"][:, :, :], mo["at"][:, :, :], mo[pick][:, :, :], ALU.mult))
                        link(dve.tensor_tensor(mo["t2"][:, :, :], mo["rank"][:, :, :], mo[pick][:, :, :], ALU.mult))
                        link(dve.reduce_sum(mo1["row1"][:, :], mo["t1"][:, :, :], AX_X))
                        link(dve.reduce_sum(mo1["row2"][:, :], mo["t2"][:, :, :], AX_X))
                        link(dve.tensor_copy(scatter_at[:, c, :], mo1["row1"][:, :]))
                        link(dve.tensor_copy(rank_of[:, c, tiles], mo1["row2"][:, :]))
                    dve.tensor_copy(mo1["row1"][:, :], mo1["row2"][:, :]).then_inc(s.scatter_ready, 1)
                    link.end()

            groups(dve, slots_step, heads_step)

            link = Chain(dve, s.table_chain, TABLE_LINKS)
            link.start(0)
            for c in range(2):
                link(dve.tensor_tensor(pad_f[:, c, :], region_at[:, :], count[:, :], ALU.add))
                link(dve.tensor_scalar(pad_f[:, c, :], pad_f[:, c, :], lane[:, c:c + 1], None, ALU.add))
            dve.tensor_copy(pad_at[:, :, :], pad_f[:, :, :]).then_inc(s.pad_ready, 1)
            steps = NT // ER
            link(dve.tensor_tensor(used[:, :, :], count[:, :].unsqueeze(2).broadcast_to([P, E, steps]),
                                   step_at[:, :].unsqueeze(1).broadcast_to([P, E, steps]), ALU.is_gt))
            link(dve.reduce_sum(tiles_of[:, :], used[:, :, :], AX_X))
            for e in range(E):
                link(dve.tensor_tensor(base_of[:, e + 1:e + 2], base_of[:, e:e + 1], tiles_of[:, e:e + 1], ALU.add))
            every = [P, EXPERT_TILES, E]
            link(dve.tensor_tensor(past[:, :, :], tile_no[:, :].unsqueeze(2).broadcast_to(every),
                                   base_of[:, 1:E + 1].unsqueeze(1).broadcast_to(every), ALU.is_ge))
            link(dve.reduce_sum(tile_e[:, :], past[:, :, :], AX_X))
            link(dve.tensor_tensor(past_w[:, :, :], past[:, :, :], tiles_of[:, :].unsqueeze(1).broadcast_to(every),
                                   ALU.mult))
            link(dve.reduce_sum(tile_b[:, :], past_w[:, :, :], AX_X))
            link(dve.tensor_scalar(tile_real[:, :], tile_e[:, :], float(E), float(ER), ALU.is_lt, ALU.mult))
            link(dve.tensor_scalar(tile_e[:, :], tile_e[:, :], float(E - 1), None, ALU.min))
            link(dve.tensor_tensor(tile_row[:, :], tile_no[:, :], tile_b[:, :], ALU.subtract))
            link(dve.tensor_tensor(tile_row[:, :], tile_row[:, :], tile_real[:, :], ALU.mult))
            link(dve.scalar_tensor_tensor(tile_row[:, :], tile_e[:, :], float(REGION), tile_row[:, :],
                                          ALU.mult, ALU.add))
            dve.tensor_copy(table[:, 1, :], tile_e[:, :])
            dve.tensor_copy(table[:, 0, :], tile_row[:, :]).then_inc(s.table_ready, 1)
            link(dve.tensor_scalar(base_rows[:, :], base_of[:, 0:E], float(ER), None, ALU.mult))
            for c in range(2):
                link(dve.tensor_tensor(place_w[:, c, :, :], pick_of[:, c, :, :],
                                       base_rows[:, :].unsqueeze(1).broadcast_to([P, TILES, E]), ALU.mult))
                link(dve.reduce_sum(place_f[:, c, :], place_w[:, c, :, :], AX_X))
            link(dve.tensor_tensor(place_f[:, :, :], place_f[:, :, :], rank_of[:, :, :], ALU.add))
            dve.tensor_copy(y_at[:, :, :], place_f[:, :, :]).then_inc(s.place_ready, 1)
            link.end()

            dve.wait_ge(s.experts_in, EXPERT_LOADS)

            def take_fc_w(p, h, j):
                e = dve.value_load(table[0:1, 1, bass.ds(j, 1)], min_val=0, max_val=E - 1)
                dve.wait_ge(fc_done[p], h)
                dve.wait_ge(gelu_done[p], h)
                dve.tensor_copy(fc_b[:, p, :], fc_b_all[:, bass.ds(e * HC, HC)])
                dve.tensor_copy(fc_w[:, p, :], fc_all[:, bass.ds(e * HID, HID)]).then_inc(fc_w_in[p], 1)

            def turn_out(p, h):
                dve.wait_ge(rows_turned[p], h + 1)
                dve.wait_ge(fc_done[p], h)
                dve.tensor_copy(rowsT[:, p, :], ROWS[p][:, 0:ER]).then_inc(rowsT_ready[p], 1)

            def y_add(p, h, j):
                e = dve.value_load(table[0:1, 1, bass.ds(j, 1)], min_val=0, max_val=E - 1)
                dve.wait_ge(proj_done[p], h + 1)
                dve.wait_ge(y_stored[p], 16 * h)
                dve.tensor_tensor(y_out[:, p, :, :], YP[p][:, 0:2 * P].rearrange("p (c d) -> p c d", c=2),
                                  proj_b_all[:, bass.ds(e, 1), :].broadcast_to([P, 2, P]), ALU.add
                                  ).then_inc(y_ready[p], 1)

            for p in range(2):
                take_fc_w(p, 0, p)
                turn_out(p, 0)

            def tile_pair(m):
                for p in range(2):
                    take_fc_w(p, m, 2 * m + p)
                    turn_out(p, m)
                    y_add(p, m - 1, 2 * m - 2 + p)

            loop(dve, 1, PAIRS, tile_pair)
            take_fc_w(0, PAIRS, 2 * PAIRS)
            turn_out(0, PAIRS)
            y_add(0, PAIRS - 1, 2 * PAIRS - 2)
            y_add(1, PAIRS - 1, 2 * PAIRS - 1)
            y_add(0, PAIRS, 2 * PAIRS)

            dve.wait_ge(s.shared_in, 64)

            def add_up(p, h, g):
                dve.wait_ge(sum_done[p], h + 1)
                dve.wait_ge(out_stored[p], 16 * h)
                dve.tensor_tensor(total[:, p, :, :], bank[4 + p][:, :].rearrange("p (b d) -> p b d", b=GB),
                                  projs_b[:, :].unsqueeze(1).broadcast_to([P, GB, P]), ALU.add
                                  ).then_inc(s.base_added, 1)
                dve.tensor_copy(gate_now[:, p, :, :], gate_of[:, :, bass.ds(g * GB, GB)]).then_inc(s.base_added, 1)
                dve.wait_ge(s.base_added, 4 * g + 2)
                dve.wait_ge(y_gathered[p], 128 * h + 128)
                for c in range(2):
                    for b in range(GB):
                        last = dve.scalar_tensor_tensor(total[:, p, b, :], y_in[:, p, c, b, :],
                                                        gate_now[:, p, c, b:b + 1], total[:, p, b, :],
                                                        ALU.mult, ALU.add)
                    if c == 0:
                        last.then_inc(s.base_added, 2)
                        dve.wait_ge(s.base_added, 4 * g + 4)
                last.then_inc(total_ready[p], 1)

            def group_pair(m):
                for p in range(2):
                    add_up(p, m, 2 * m + p)

            loop(dve, 0, NG // 2, group_pair)

        @block.tensor
        def _(pe):
            def mm(dst, w, rhs, start=True, stop=True):
                return pe.matmul(dst, w, rhs, start=start, stop=stop)

            pe.wait_ge(s.consts_made, CONSTS)
            pe.wait_ge(s.columns_in, 16 * 9)
            pe.transpose(bank[7][:, 0:13], vec_rows[:, :], ident[0:13, 0:13]).then_inc(s.columns_turned, 1)
            pe.wait_ge(s.weights_in, 16 * 14)
            for j in range(13):
                last = pe.transpose(bank[j // 4][:, (j % 4) * P:(j % 4 + 1) * P], NAT[:, 3 + j, :], ident[:, :])
                if j % 4 == 3:
                    last.then_inc(s.turned_w, 1)
            pe.transpose(bank[3][:, P:P + E], NAT[0:E, 16, :], ident[0:E, 0:E]).then_inc(s.turned_w, 1)
            mm(bank[4][:, 0:P], NAT[:, 0, :], NAT[:, 1, :]).then_inc(s.fused_w, 1)
            pe.wait_ge(s.turned_w_out, 1)
            mm(bank[5][:, 0:3 * P], NAT[:, 2, :], WIH).then_inc(s.fused_w, 1)
            pe.wait_ge(s.weights_ready, 6)
            pe.wait_ge(s.turned_w_out, 2)
            mm(bank[6][:, 0:1], WO_T, col[:, BV:BV + 1]).then_inc(s.fused_w, 1)
            pe.wait_ge(s.weights_ready, 9)

            def slots_step(t, step, i=0):
                n = 3 * t + i
                if step == "turn":
                    pe.wait_ge(s.x2_ready, t)
                    pe.wait_ge(s.xln_ready, t + 1)
                    for b in range(GB):
                        last = pe.transpose(G3[:, b * P:(b + 1) * P], xln[:, b, :], ident[:, :])
                    last.then_inc(s.turned, 1)
                    pe.wait_ge(s.ctx_in, 16 * t + 16)
                    for b in range(GB):
                        last = pe.transpose(G0[:, b * M:(b + 1) * M], ctx_tok[:, b, :], ident[0:M, 0:M])
                    last.then_inc(s.turned, 1)
                    for b in range(GB):
                        last = pe.transpose(G2[:, b * P:(b + 1) * P], x_tok[:, b, :], ident[:, :])
                    last.then_inc(s.turned, 1)
                if step == "keys":
                    pe.wait_ge(s.ctxT_ready, t + 1)
                    mm(G1[:, 0:CM], KQ_W[:, :], ctxT[:, :]).then_inc(s.keys_done, 1)
                    for b, dst in enumerate((G0, G2, G3, G1)):
                        if b == 1:
                            pe.wait_ge(s.xT_ready, t + 1)
                        if b == 3:
                            pe.wait_ge(s.keys_ready, t + 1)
                        mm(dst[0:M, 0:3 * P], ctxT[:, b * M:(b + 1) * M], VG_W[:, :]).then_inc(s.values_done, 1)
                if step == "score":
                    pe.wait_ge(s.squared, n + 1)
                    if i == 0:
                        pe.wait_ge(s.values_by_act, 2 * t + 2)
                        pe.wait_ge(s.values_by_dve, 2 * t + 2)
                    mm(G1[0:M, :], mean_w[:, 0:M], slot_sq[:, :]).then_inc(s.sumsq_done, 1)
                    for b in range(GB):
                        last = mm(G0[0:M, b * P:(b + 1) * P], keysT[:, b * M:(b + 1) * M],
                                  slots[:, b * P:(b + 1) * P])
                    last.then_inc(s.scored, 1)
                    mm(G3[:, :], WHH[:, 0, :], slots[:, :], stop=False)
                if step == "share":
                    pe.wait_ge(s.slot_r_ready, n + 1)
                    mm(G1[:, :], WHH[:, 1, :], slots[:, :], stop=False)
                    pe.wait_ge(s.rz_ready, n + 1)
                    for b in range(GB):
                        last = mm(G2[0:M, b * P:(b + 1) * P], prob_rz[0:M + 1, b:b + 1].broadcast_to([M + 1, M]),
                                  prob[0:M + 1, b * P:(b + 1) * P])
                    last.then_inc(s.share_summed, 1)
                if step == "gates":
                    pe.wait_ge(s.share_sum_read, n + 1)
                    mm(G2[:, :], WHH[:, 2, :], slots[:, :]).then_inc(s.hn_done, 1)
                    pe.wait_ge(s.share_ready, n + 1)
                    for gate, dst, done in ((0, G3, s.r_done), (2, G0, s.xn_done), (1, G1, s.z_done)):
                        for b in range(GB):
                            last = pe.matmul(dst[:, b * P:(b + 1) * P], values[:, b, gate * P:(gate + 1) * P],
                                             share[:, b * P:(b + 1) * P], start=(gate == 2),
                                             stop=(gate == 2 or b == GB - 1))
                        last.then_inc(done, 1)
                if step == "center":
                    pe.wait_ge(s.x1_ready, t + 1)
                    mm(G0[:, :], center_w[:, :], x1[:, :]).then_inc(s.c1_done, 1)
                if step == "spread":
                    pe.wait_ge(s.c1_squared, t + 1)
                    mm(G1[:, :], mean_w[:, :], c1_sq[:, :]).then_inc(s.v1_done, 1)
                if step == "route":
                    pe.wait_ge(s.xn1_ready, t + 1)
                    for b in range(GB):
                        last = mm(G2[:, b * E:(b + 1) * E], xn1[:, b * P:(b + 1) * P], RT[:, :])
                    last.then_inc(s.logits1_done, 1)
                    mm(G3[:, :], A0_T, xn1[:, :]).then_inc(s.down_done, 1)
                    mm(G1[:, :], W0_T, xn1[:, :], stop=False)
                if step == "turn_gate":
                    pe.wait_ge(s.gate_ready, t + 1)
                    for b in range(GB):
                        last = pe.transpose(G0[:, b * P:(b + 1) * P], gate_x[:, b, :, :].rearrange("p e r -> p (e r)"),
                                            ident[:, :])
                    last.then_inc(s.gate_turned, 1)
                if step == "out":
                    pe.wait_ge(s.down_ready, t + 1)
                    mm(G1[:, :], LB_T, down[:, :], start=False).then_inc(s.ffn1_done, 1)

            def heads_step(a, step, k=0):
                n = UNITS * a + k
                if step == "norm":
                    pe.wait_ge(s.x2_ready, a + 1)
                    pe.wait_ge(s.scatter_ready, a)
                    pe.wait_ge(s.xn3_tok_ready, a)
                    mm(BS[:, :], center_w[:, :], x2[:, :]).then_inc(s.c2_done, 1)
                    pe.wait_ge(s.c2_squared, a + 1)
                    mm(BT[:, :], mean_w[:, :], c2_sq[:, :]).then_inc(s.v2_done, 1)
                if step == "project":
                    for b in range(GB):
                        last = mm(BO[0:M, b * P:(b + 1) * P], ctxT[:, b * M:(b + 1) * M], WV_T)
                    last.then_inc(s.v_done, 1)
                    pe.wait_ge(s.xn2_ready, a + 1)
                    mm(BT[:, 0:CM], WK_T, ctxT[:, :]).then_inc(s.k_done, 1)
                    mm(BS[:, :], WQ_T, xn2[:, :]).then_inc(s.q_done, 1)
                if step == "unit":
                    if k < UNITS:
                        b, u = k // 4, k % 4
                        if k == 0:
                            pe.wait_ge(s.k_ready, a + 1)
                        if k < 4:
                            pe.wait_ge(s.q_masked, 4 * a + k + 1)
                        if k > 0:
                            pe.wait_ge(s.head_shifted, n)
                        mm(BS[:, 0:Q * M], q_mask[:, u, b * P:(b + 1) * P],
                           k_quad[:, b, :, :].rearrange("p g m -> p (g m)")).then_inc(s.head_scored, 1)
                    if 1 <= k <= UNITS:
                        j = k - 1
                        pe.wait_ge(s.head_exp, UNITS * a + j + 1)
                        if j > 0:
                            pe.wait_ge(s.head_pT_ready, UNITS * a + j)
                        for g in range(Q):
                            last = pe.transpose(BT[0:M, g * P:(g + 1) * P], head_p[:, j % 2, g, :], ident[:, :])
                        last.then_inc(s.head_turned, 1)
                    if k >= 2:
                        j = k - 2
                        b, u = j // 4, j % 4
                        pe.wait_ge(s.head_pT_ready, UNITS * a + j + 1)
                        if j == 0:
                            pe.wait_ge(s.v_ready, a + 1)
                        for bnk, w in ((BO, None), (BZ, sum_w)):
                            for g in range(Q):
                                lhs = v_pad[:, b * Q + g, 32 * u:32 * u + 32] if w is None else sum_w[0:M, u, :]
                                last = pe.matmul(bnk[32 * g:32 * g + 32, b * P:(b + 1) * P], lhs,
                                                 head_pT[:, j % 2, g * P:(g + 1) * P],
                                                 start=(u == 0), stop=(u == 3))
                        last.then_inc(s.head_summed, 1)
                if step == "mix":
                    pe.wait_ge(s.attended, a + 1)
                    mm(BS[:, :], WO_T, o_all[:, :]).then_inc(s.wo_done, 1)
                if step == "center":
                    pe.wait_ge(s.x3_ready, a + 1)
                    mm(BT[:, :], center_w[:, :], x3[:, :]).then_inc(s.c3_done, 1)
                if step == "spread":
                    pe.wait_ge(s.c3_squared, a + 1)
                    mm(BZ[:, :], mean_w[:, :], c3_sq[:, :]).then_inc(s.v3_done, 1)
                if step == "route":
                    pe.wait_ge(s.xn3_ready, a + 1)
                    for b in range(GB):
                        last = mm(BO[:, b * E:(b + 1) * E], xn3[:, b * P:(b + 1) * P], WR[:, :])
                    last.then_inc(s.logits2_done, 1)
                    for b in range(GB):
                        last = pe.transpose(BT[:, b * P:(b + 1) * P], xn3[:, b * P:(b + 1) * P], ident[:, :])
                    last.then_inc(s.xn3_turned, 1)
                if step == "rank":
                    pe.wait_ge(s.both_ready, a + 1)
                    both = mo["both"][:, :, :].rearrange("p b e -> p (b e)")
                    mm(BS[:, 0:GB * E], before[:, :], both)
                    mm(BS[:, GB * E:2 * GB * E], ones[:, :], both).then_inc(s.ranks_done, 1)

            groups(pe, slots_step, heads_step)

            pe.wait_ge(s.x2_ready, NG)
            pe.wait_ge(s.scatter_ready, NG)
            pe.wait_ge(s.xn3_tok_ready, NG)

            def turn(p, h):
                pe.wait_ge(rows_in[p], 16 * h + 16)
                pe.wait_ge(rowsT_ready[p], h)
                for c in range(2):
                    last = pe.transpose(ROWS[p][:, c * P:(c + 1) * P], rows[:, p, c, :], ident[:, :])
                last.then_inc(rows_turned[p], 1)

            def fc(p, h):
                pe.wait_ge(rowsT_ready[p], h + 1)
                pe.wait_ge(fc_w_in[p], h + 1)
                pe.wait_ge(gelu_done[p], h)
                for c in range(HC):
                    last = mm(FC[p][c // 2][:, (c % 2) * ER:(c % 2 + 1) * ER], fc_w[:, p, c:HID:HC], rowsT[:, p, :])
                last.then_inc(fc_done[p], 1)

            def proj(p, h):
                pe.wait_ge(gelu_done[p], h + 1)
                pe.wait_ge(proj_w_in[p], h + 1)
                pe.wait_ge(y_ready[p], h)
                for i in range(2):
                    for c in range(HC):
                        last = mm(YP[p][:, i * P:(i + 1) * P], hidden[:, p, c, i * P:(i + 1) * P],
                                  proj_w[:, p, c * P:(c + 1) * P], start=(c == 0), stop=(c == HC - 1))
                last.then_inc(proj_done[p], 1)

            turn(0, 0)
            turn(1, 0)
            fc(0, 0)
            def tile_pair(m):
                turn(0, m)
                fc(1, m - 1)
                proj(0, m - 1)
                turn(1, m)
                fc(0, m)
                proj(1, m - 1)

            loop(pe, 1, PAIRS, tile_pair)
            turn(0, PAIRS)
            fc(1, PAIRS - 1)
            proj(0, PAIRS - 1)
            fc(0, PAIRS)
            proj(1, PAIRS - 1)
            proj(0, PAIRS)

            pe.wait_ge(s.shared_in, 64)
            for p in range(2):
                pe.wait_ge(gelu_done[p], PAIRS + 1 - p)
                pe.wait_ge(y_ready[p], PAIRS + 1 - p)

            def fc_shared(p, h, first=False):
                pe.wait_ge(c_in[p], 32 * h + 32)
                for c in range(HC):
                    if p == 1:
                        pe.wait_ge(gelu_s_done[0], HC * h + c + 1)
                    elif not first:
                        pe.wait_ge(gelu_s_done[1], HC * h - HC + c + 1)
                    mm(bank[c][:, :], fcs_w[:, c:HID:HC], xn3_in[:, p, :]).then_inc(s.fc_s_done, 1)

            def sum_shared(p, h):
                pe.wait_ge(gelu_s_done[p], HC * h + HC)
                pe.wait_ge(total_ready[p], h)
                for b in range(GB):
                    cols = slice(b * P, (b + 1) * P)
                    mm(bank[4 + p][:, cols], x3_in[:, p, cols], ident[:, :], stop=False)
                    for c in range(HC):
                        last = mm(bank[4 + p][:, cols], hidden_s[:, p, c, cols], projs_w[:, c, :],
                                  start=False, stop=(c == HC - 1))
                last.then_inc(sum_done[p], 1)

            fc_shared(0, 0, first=True)
            fc_shared(1, 0)
            sum_shared(0, 0)
            def group_pair(m):
                fc_shared(0, m)
                sum_shared(1, m - 1)
                fc_shared(1, m)
                sum_shared(0, m)

            loop(pe, 1, NG // 2, group_pair)
            sum_shared(1, NG // 2 - 1)


_INS = ['x', 'ctx_1024', 'L0_xattn_Wq', 'L0_xattn_Wk', 'L0_xattn_Wv', 'L0_xattn_gru_wih', 'L0_xattn_gru_whh',
        'L0_xattn_gru_bih', 'L0_xattn_gru_bhh', 'L0_xattn_slot_norm_w', 'L0_xattn_input_norm_w', 'L0_ffn_W',
        'L0_ffn_b', 'L0_ffn_R', 'L0_ffn_A', 'L0_ffn_B', 'L1_xattn_Wq', 'L1_xattn_bq', 'L1_xattn_Wk', 'L1_xattn_bk',
        'L1_xattn_Wv', 'L1_xattn_bv', 'L1_xattn_Wo', 'L1_xattn_bo', 'L1_ffn_Wfc_s', 'L1_ffn_bfc_s',
        'L1_ffn_Wproj_s', 'L1_ffn_bproj_s', 'L1_ffn_Wr', 'L1_ffn_Wfc', 'L1_ffn_bfc', 'L1_ffn_Wproj', 'L1_ffn_bproj']
_OUTS = [((64, 128, 128), 'float32')]


def kernel(**inputs):
    import numpy as _np
    import concourse.bacc as _bacc
    from concourse import mybir as _mybir
    from concourse.bass_utils import run_bass_kernel_spmd as _run

    nc = _bacc.Bacc("TRN2", target_bir_lowering=False, num_devices=1)
    arrays, args = {}, []
    for name in _INS:
        a = _np.ascontiguousarray(inputs[name])
        arrays[f"in_{name}_dram"] = a
        args.append(nc.dram_tensor(f"in_{name}_dram", a.shape, _mybir.dt.from_np(a.dtype), kind="ExternalInput").ap())
    for i, (shape, dtype) in enumerate(_OUTS):
        dt = _mybir.dt.from_np(_np.dtype(dtype))
        args.append(nc.dram_tensor(f"out_{i}_dram", shape, dt, kind="ExternalOutput").ap())
    two_layers(nc, *args)
    r = _run(nc, [arrays], core_ids=[0])
    got = tuple(r.results[0][f"out_{i}_dram"] for i in range(len(_OUTS)))
    return got[0]
```

```python
from contextlib import ExitStack

import numpy as np

import concourse.bass as bass
from concourse import mybir

F32 = mybir.dt.float32
I32 = mybir.dt.int32
ALU = mybir.AluOpType
ACT = mybir.ActivationFunctionType
AX_X = mybir.AxisListType.X

P = 128
GB = 4
GT = GB * P
CONSTS = 33
SLOTS_LINKS = 28
HEADS_LINKS = 16
TAIL_LINKS = 19
TABLE_LINKS = 25
UNITS = 16
ER = 256
LN_SET = "natural_log_exp_and_others"
TANH_SET = "exp_and_others"
RMS_EPS = 1e-6
LN_EPS = 1e-5

STEPS = [
    ("slots", "turn"), ("heads", "norm"), ("late", "spread"), ("heads", "norm_spread"), ("slots", "keys"),
    ("late", "route"), ("slots", "score", 0), ("heads", "project"), ("late", "rank"), ("slots", "recur", 0),
    ("slots", "probs", 0), ("heads", "unit_score", 0), ("slots", "share_sum", 0), ("slots", "hidden", 0),
    ("slots", "share", 0), ("heads", "unit_score", 1), ("heads", "unit_turn", 0), ("slots", "gates", 0),
    ("heads", "unit_turn", 1), ("slots", "cell", 0), ("heads", "unit_score", 2), ("slots", "update", 0),
    ("slots", "score", 1), ("slots", "recur", 1), ("heads", "unit_attend", 0), ("slots", "probs", 1),
    ("heads", "unit_score", 3), ("heads", "unit_turn", 2), ("slots", "share_sum", 1), ("slots", "hidden", 1),
    ("heads", "unit_attend", 1), ("heads", "unit_score", 4), ("heads", "unit_attend", 2), ("slots", "share", 1),
    ("ahead", "stats"), ("heads", "unit_turn", 3), ("heads", "unit_score", 5), ("slots", "gates", 1),
    ("heads", "unit_turn", 4), ("heads", "unit_score", 6), ("slots", "cell", 1), ("slots", "update", 1),
    ("heads", "unit_attend", 3), ("heads", "unit_attend", 4), ("heads", "unit_turn", 5), ("heads", "unit_score", 7),
    ("ahead", "normal"), ("slots", "score", 2), ("heads", "unit_turn", 6), ("slots", "recur", 2),
    ("heads", "unit_score", 8), ("heads", "unit_attend", 5), ("heads", "unit_turn", 7), ("heads", "unit_score", 9),
    ("heads", "unit_attend", 6), ("slots", "probs", 2), ("heads", "unit_turn", 8), ("heads", "unit_attend", 7),
    ("slots", "share_sum", 2), ("heads", "unit_score", 10), ("slots", "hidden", 2), ("heads", "unit_turn", 9),
    ("slots", "share", 2), ("heads", "unit_attend", 8), ("heads", "unit_score", 11), ("slots", "gates", 2),
    ("slots", "cell", 2), ("heads", "unit_turn", 10), ("heads", "unit_attend", 9), ("heads", "unit_score", 12),
    ("slots", "update", 2), ("heads", "unit_turn", 11), ("heads", "unit_attend", 10), ("heads", "unit_score", 13),
    ("heads", "unit_turn", 12), ("heads", "unit_attend", 11), ("heads", "unit_score", 14),
    ("heads", "unit_turn", 13), ("heads", "unit_attend", 12), ("slots", "center"), ("heads", "unit_score", 15),
    ("heads", "unit_turn", 14), ("slots", "spread"), ("heads", "unit_attend", 13), ("heads", "unit_turn", 15),
    ("heads", "unit_attend", 14), ("heads", "unit_attend", 15), ("slots", "route"), ("heads", "mix"),
    ("slots", "gate"), ("next", "keys"), ("slots", "turn_gate"), ("heads", "residual"), ("slots", "out"),
    ("heads", "center"), ("ahead", "context_stats"), ("next", "keys_out"),
]


class Signals:
    def __init__(self, sem):
        self.table_chain = sem("table_chain")
        self.table_ready = sem("table_ready")
        self.pad_ready = sem("pad_ready")
        self.place_ready = sem("place_ready")
        self.experts_in = sem("experts_in")
        self.shared_in = sem("shared_in")
        self.y_now_ready = sem("y_now_ready")
        self.base_added = sem("base_added")
        self.waits_over = sem("waits_over")
        self.weights_in = sem("weights_in")
        self.columns_in = sem("columns_in")
        self.tail_chain = sem("tail_chain")
        self.consts_made = sem("consts_made")
        self.turned_w = sem("turned_w")
        self.turned_w_out = sem("turned_w_out")
        self.fused_w = sem("fused_w")
        self.weights_ready = sem("weights_ready")
        self.x_in = sem("x_in")
        self.ctx_in = sem("ctx_in")
        self.ctx_squared = sem("ctx_squared")
        self.ctx_ms_ready = sem("ctx_ms_ready")
        self.var_ready = sem("var_ready")
        self.stats_ready = sem("stats_ready")
        self.roots_ready = sem("roots_ready")
        self.share_ln = sem("share_ln")
        self.share_rz_ready = sem("share_rz_ready")
        self.hn_biased = sem("hn_biased")
        self.z_gate_ready = sem("z_gate_ready")
        self.kept_ready = sem("kept_ready")
        self.o_ln = sem("o_ln")
        self.o_rz_ready = sem("o_rz_ready")
        self.slot_ln = sem("slot_ln")
        self.v1_ln = sem("v1_ln")
        self.v2_ln = sem("v2_ln")
        self.v3_ln = sem("v3_ln")
        self.rs1_ready = sem("rs1_ready")
        self.rs2_ready = sem("rs2_ready")
        self.rs3_ready = sem("rs3_ready")
        self.ctx_scale = sem("ctx_scale")
        self.xln_ready = sem("xln_ready")
        self.turned = sem("turned")
        self.slots_in = sem("slots_in")
        self.ctxT_ready = sem("ctxT_ready")
        self.xT_ready = sem("xT_ready")
        self.keys_done = sem("keys_done")
        self.keys_ready = sem("keys_ready")
        self.values_done = sem("values_done")
        self.values_by_act = sem("values_by_act")
        self.values_by_dve = sem("values_by_dve")
        self.squared = sem("squared")
        self.scored = sem("scored")
        self.sumsq_done = sem("sumsq_done")
        self.slot_r_ready = sem("slot_r_ready")
        self.score_read = sem("score_read")
        self.bias_ready = sem("bias_ready")
        self.exp_done = sem("exp_done")
        self.rz_ready = sem("rz_ready")
        self.share_summed = sem("share_summed")
        self.share_ready = sem("share_ready")
        self.hn_done = sem("hn_done")
        self.r_done = sem("r_done")
        self.xn_done = sem("xn_done")
        self.z_done = sem("z_done")
        self.r_tanh_ready = sem("r_tanh_ready")
        self.z_tanh_ready = sem("z_tanh_ready")
        self.cell_ready = sem("cell_ready")
        self.n_ready = sem("n_ready")
        self.slots_new = sem("slots_new")
        self.x1_ready = sem("x1_ready")
        self.c1_done = sem("c1_done")
        self.c1_squared = sem("c1_squared")
        self.v1_done = sem("v1_done")
        self.xn1_ready = sem("xn1_ready")
        self.logits1_done = sem("logits1_done")
        self.down_done = sem("down_done")
        self.gate_shifted = sem("gate_shifted")
        self.gate_exp = sem("gate_exp")
        self.gate_ready = sem("gate_ready")
        self.gate_turned = sem("gate_turned")
        self.gate_T_ready = sem("gate_T_ready")
        self.down_ready = sem("down_ready")
        self.ffn1_done = sem("ffn1_done")
        self.x2_ready = sem("x2_ready")
        self.slots_chain = sem("slots_chain")
        self.stats_chain = sem("stats_chain")
        self.c2_done = sem("c2_done")
        self.c2_squared = sem("c2_squared")
        self.v2_done = sem("v2_done")
        self.xn2_ready = sem("xn2_ready")
        self.q_done = sem("q_done")
        self.k_done = sem("k_done")
        self.v_done = sem("v_done")
        self.q_by_act = sem("q_by_act")
        self.q_by_dve = sem("q_by_dve")
        self.k_ready = sem("k_ready")
        self.v_ready = sem("v_ready")
        self.head_scored = sem("head_scored")
        self.head_shifted = sem("head_shifted")
        self.head_exp = sem("head_exp")
        self.head_turned = sem("head_turned")
        self.head_pT_ready = sem("head_pT_ready")
        self.head_summed = sem("head_summed")
        self.attended = sem("attended")
        self.wo_done = sem("wo_done")
        self.x3_ready = sem("x3_ready")
        self.c3_done = sem("c3_done")
        self.c3_squared = sem("c3_squared")
        self.v3_done = sem("v3_done")
        self.xn3_ready = sem("xn3_ready")
        self.logits2_done = sem("logits2_done")
        self.xn3_turned = sem("xn3_turned")
        self.xn3_tok_ready = sem("xn3_tok_ready")
        self.gap_ready = sem("gap_ready")
        self.gap_exp = sem("gap_exp")
        self.both_ready = sem("both_ready")
        self.ranks_done = sem("ranks_done")
        self.scatter_ready = sem("scatter_ready")
        self.heads_chain = sem("heads_chain")
        self.scattered = sem("scattered")
        self.x3_stored = sem("x3_stored")
        self.xn3_stored = sem("xn3_stored")


def two_layers(nc, x, ctx, wq0, wk0, wv0, wih, whh, bih, bhh, slot_w, in_w, w0, b0, r0, a0, lb0,
               wq1, bq1, wk1, bk1, wv1, bv1, wo1, bo1, wfc_s, bfc_s, wproj_s, bproj_s, wr, wfc, bfc,
               wproj, bproj, out):
    NB, S, D = x.shape
    M = ctx.shape[1]
    E = wr.shape[1]
    R = a0.shape[1]
    HID = wfc_s.shape[1]
    HC = HID // P
    NT = NB * S
    TILES = NT // P
    GROUPS = NB // GB
    NG = GROUPS
    CM = GB * M
    NH, DK = 16, D // 16
    Q = P // 32
    SCALE = float(D) ** -0.5
    HSCALE = float(DK) ** -0.5
    REGION = NT + ER
    EXPERT_TILES = (2 * NT + E * (ER - 1)) // ER
    assert S == P and D == P and E * R == P and NH == 4 * Q

    stack = ExitStack()
    with stack:
        def sb(name, shape, dt=F32):
            return stack.enter_context(nc.sbuf_tensor(name, shape, dt))

        def sem(name):
            return stack.enter_context(nc.semaphore(name))

        bank = [stack.enter_context(nc.psum_tensor(f"bank{i}", [P, 512], F32)) for i in range(8)]
        G0, G1, G2, G3, BS, BT, BO, BZ = bank

        x3_dram = nc.dram_tensor("x3_scratch", [P, NT], F32, kind="Internal").ap()
        xn3_dram = nc.dram_tensor("xn3_scratch", [P, NT], F32, kind="Internal").ap()
        rows_dram = nc.dram_tensor("expert_rows", [E * REGION, D], F32, kind="Internal").ap()
        y_dram = nc.dram_tensor("expert_out", [EXPERT_TILES * ER, D], F32, kind="Internal").ap()
        ends_dram = nc.dram_tensor("tile_table", [2, P], I32, kind="Internal").ap()

        NAT = sb("nat", [P, 17, P])
        TW = sb("turned_w", [P, 13, P])
        RT = sb("r0_turned", [P, E])
        WR = sb("wr", [P, E])
        KQ_W = sb("kq_w", [P, P])
        VG_W = sb("vg_w", [P, 3 * P])
        ident = sb("ident", [P, P])
        mean_w = sb("mean_w", [P, P])
        center_w = sb("center_w", [P, P])
        ones = sb("ones", [P, P])
        before = sb("before", [P, P])
        quad_mask = sb("quad_mask", [P, 4])
        quad_sel = sb("quad_sel", [P, 4, Q])
        earlier = sb("earlier", [P, E, E])
        region_at = sb("region_at", [P, E])
        region_i = sb("region_i", [P, E], I32)
        sum_w = sb("sum_w", [P, 4, 32])
        vec_rows = sb("vec_rows", [13, P])
        col = sb("columns", [P, 13])
        IH, HH, SLOT_W, IN_W, B0, BQ, BK, BV, BO1 = 0, 3, 6, 7, 8, 9, 10, 11, 12
        half_b = sb("half_b", [P, 2])
        bq_mask = sb("bq_mask", [P, 4])
        bo_all = sb("bo_all", [P, 1])
        WIH, WHH = TW[:, 0:3, :], TW[:, 3:6, :]
        W0_T, A0_T, LB_T, WQ_T, WK_T, WV_T, WO_T = (TW[:, i, :] for i in range(6, 13))

        scratch = sb("scratch", [P, 20 * GT])
        taken = [0]

        def share_a(partitions=P):
            taken[0] += GT
            return scratch[0:partitions, taken[0] - GT:taken[0]]

        x_tok = sb("x_tok", [P, GB, P])
        ctx_tok = sb("ctx_tok", [M, GB, P])
        stats = sb("stats", [P, GB, 6])
        mv = sb("mv", [P, GB, 2])
        var_tok = sb("var_tok", [P, GB])
        power = sb("power", [P, GB])
        rs_tok = sb("rs_tok", [P, GB])
        xln = sb("xln", [P, GB, P])
        ctx_sq = sb("ctx_sq", [M, GB, P])
        ctx_ms = sb("ctx_ms", [M, GB])
        ctx_r = sb("ctx_r", [M, GB])
        ctx_sc = sb("ctx_sc", [M, GB])
        ctx_nsc = sb("ctx_nsc", [M, GB])
        slots = sb("slots", [P, GT])
        xT = sb("xT", [P, GT])
        ctxT = sb("ctxT", [P, CM])
        keysT = sb("keysT", [P, CM])
        values = sb("values", [M, GB, 3 * P])
        slot_sq = share_a()
        slot_r = share_a(M)
        slot_ln = share_a(M)
        ln_buf = sb("ln_buf", [P, 2, GT])
        rms_eps = sb("rms_eps", [P, 1])
        ln_eps = sb("ln_eps", [P, 1])
        score = share_a(M)
        score_max = sb("score_max", [M, GB])
        score_b = sb("score_b", [M, GB])
        prob = sb("prob", [P, GT])
        prob_sum = sb("prob_sum", [M, GB])
        prob_rz = sb("prob_rz", [P, GB])
        share_rz = share_a(M)
        prob_n = share_a(M)
        share = share_a(M)
        r_tanh = share_a()
        z_tanh = share_a()
        hn = share_a()
        hn_part = share_a()
        n_pre = share_a()
        n_new = share_a()
        z_gate = share_a()
        n_share = share_a()
        n_taken = hn_part
        kept = share_a()
        x1 = sb("x1", [P, GT])
        c1_sq = share_a()
        rs1 = share_a()
        xn1 = share_a()
        top = {k: sb("top_" + k, [P, GB, E]) for k in ("logits", "place", "both", "e", "low")}
        top_vs = {k: sb("top_vs_" + k, [P, GB, E, E]) for k in ("above", "equal")}
        top1 = {k: sb("top1_" + k, [P, GB]) for k in ("max", "z", "s", "g")}
        gate_x = sb("gate_x", [P, GB, E, R])
        gate_T = rs1
        down = share_a()
        x2 = sb("x2", [P, GT])

        c2_sq = sb("c2_sq", [P, GT])
        rs2 = sb("rs2", [P, GT])
        xn2 = sb("xn2", [P, GT])
        q_mask = sb("q_mask", [P, 4, GT])
        k_quad = sb("k_quad", [P, GB, Q, M])
        v_pad = sb("v_pad", [M, GB * Q, 4 * (32 + DK)])
        head_max = sb("head_max", [P, 2, Q])
        head_s = sb("head_s", [P, 2, Q, M])
        head_p = sb("head_p", [P, 2, Q, M])
        head_pT = sb("head_pT", [M, 2, Q * P])
        o_rz = sb("o_rz", [P, GT])
        o_all = sb("o_all", [P, GT])
        x3 = sb("x3", [P, GT])
        c3_sq = sb("c3_sq", [P, GT])
        rs3 = sb("rs3", [P, GT])
        xn3 = sb("xn3", [P, GT])
        xn3_tok = sb("xn3_tok", [P, GB, P])
        mo = {k: sb("moe_" + k, [P, GB, E]) for k in ("logits", "place", "both", "rank", "at", "sign")}
        mo_vs = {k: sb("moe_vs_" + k, [P, GB, E, E]) for k in ("above", "equal")}
        mo2 = {k: sb("moe2_" + k, [P, 2, GB, E]) for k in ("pick", "at", "rank")}
        mo1 = {k: sb("moe1_" + k, [P, GB]) for k in ("d", "e", "s")}
        scatter_f = sb("scatter_f", [P, 2, GB])
        count = sb("count", [P, E])
        scatter_at = sb("scatter_at", [P, 2, GB], I32)
        gate_of = sb("gate_of", [P, 2, TILES])
        rank_of = sb("rank_of", [P, 2, TILES])
        pick_of = sb("pick_of", [P, 2, TILES, E])

        zeros = sb("zeros", [P, P])
        step_i = sb("step_i", [P, NT // ER], I32)
        step_at = sb("step_at", [P, NT // ER])
        tile_i = sb("tile_i", [P, EXPERT_TILES], I32)
        tile_no = sb("tile_no", [P, EXPERT_TILES])
        used = sb("used", [P, E, NT // ER])
        tiles_of = sb("tiles_of", [P, E])
        base_of = sb("base_of", [P, E + 1])
        past = sb("past", [P, EXPERT_TILES, E])
        past_w = sb("past_w", [P, EXPERT_TILES, E])
        tile_e = sb("tile_e", [P, EXPERT_TILES])
        tile_b = sb("tile_b", [P, EXPERT_TILES])
        tile_real = sb("tile_real", [P, EXPERT_TILES])
        tile_row = sb("tile_row", [P, EXPERT_TILES])
        table = sb("table", [P, 2, EXPERT_TILES], I32)
        pad_at = sb("pad_at", [P, E], I32)
        base_rows = sb("base_rows", [P, E])
        place_w = sb("place_w", [P, 2, TILES, E])
        place_f = sb("place_f", [P, 2, TILES])
        y_at = sb("y_at", [P, 2, TILES], I32)
        y_now = sb("y_now", [P, 2, 2, GB], I32)
        rows = sb("rows", [P, 2, 2, P])
        rowsT = sb("rowsT", [P, 2, ER])
        fc_w = sb("fc_w", [P, 2, HID])
        fc_b = sb("fc_b", [P, 2, HC])
        proj_w = sb("proj_w", [P, 2, HC * P])
        fc_all = scratch[:, 0:E * HID]
        proj_all = scratch[:, E * HID:2 * E * HID]
        fc_b_all = sb("fc_b_all", [P, E * HC])
        proj_b_all = sb("proj_b_all", [P, E, P])
        hidden = sb("hidden", [P, 2, HC, ER])
        y_out = sb("y_out", [P, 2, 2, P])
        fcs_w = sb("fcs_w", [P, HID])
        fcs_b = sb("fcs_b", [P, HC])
        projs_w = sb("projs_w", [P, HC, P])
        projs_b = sb("projs_b", [P, P])
        xn3_in = scratch[:, 0:2 * GT].rearrange("p (i n) -> p i n", i=2)
        x3_in = scratch[:, 2 * GT:4 * GT].rearrange("p (i n) -> p i n", i=2)
        hidden_s = scratch[:, 4 * GT:4 * GT + 2 * HC * GT].rearrange("p (i c n) -> p i c n", i=2, c=HC)
        y_in = scratch[:, 12 * GT:16 * GT].rearrange("p (i c b d) -> p i c b d", i=2, c=2, b=GB)
        gate_now = sb("gate_now", [P, 2, 2, GB])
        total = scratch[:, 16 * GT:18 * GT].rearrange("p (i b d) -> p i b d", i=2, b=GB)

        def pair(name):
            return [sem(f"{name}{i}") for i in range(2)]

        rows_in, rows_turned, rowsT_ready, fc_w_in, fc_done, gelu_done = map(
            pair, ("rows_in", "rows_turned", "rowsT_ready", "fc_w_in", "fc_done", "gelu_done"))
        proj_w_in, proj_done, y_ready, y_stored = map(pair, ("proj_w_in", "proj_done", "y_ready", "y_stored"))
        c_xn3_in, c_x3_in, fc_s_done, y_gathered, gelu_s_done, sum_done, total_ready, out_stored = map(
            pair, ("c_xn3_in", "c_x3_in", "fc_s_done", "y_gathered", "gelu_s_done", "sum_done", "total_ready", "out_stored"))

        s = Signals(sem)

        block = stack.enter_context(nc.Block())

        def loop(eng, first, end, body):
            body(first)
            if first + 1 < end:
                with eng.Fori(first + 1, end) as i:
                    body(i)

        def groups(eng, slots_step, heads_step):
            def turn(t, ahead=True, slots=True, heads=True, late=True):
                for stream, step, *k in STEPS:
                    if stream == "ahead" and ahead:
                        slots_step(t + 1, step, *k)
                    if stream == "slots" and slots:
                        slots_step(t, step, *k)
                    if stream == "next" and slots:
                        heads_step(t, step, *k)
                    if stream == "heads" and heads:
                        heads_step(t - 1, step, *k)
                    if stream == "late" and late:
                        heads_step(t - 2, step, *k)

            for stream, step, *k in STEPS:
                if stream == "ahead":
                    slots_step(0, step, *k)
            turn(0, heads=False, late=False)
            turn(1, late=False)
            loop(eng, 2, NG - 1, turn)
            turn(NG - 1, ahead=False)
            turn(NG, ahead=False, slots=False)
            turn(NG + 1, ahead=False, slots=False, heads=False)

        FC = [(G0, G1), (G2, G3)]
        ROWS = [BS, BT]
        YP = [BO, BZ]
        EXPERT_LOADS = 16 * (2 * E + 2)
        PAIRS = EXPERT_TILES // 2
        assert EXPERT_TILES % 2 == 1 and NG % 2 == 0

        def wait_apart(eng, *waits):
            for signal, value in waits:
                eng.wait_ge(signal, value)
            eng.sem_inc(s.waits_over)

        class Chain:
            def __init__(self, eng, done, per):
                self.eng, self.done, self.per, self.n = eng, done, per, 0

            def start(self, t):
                self.base, self.n = t * self.per, 0

            def __call__(self, instruction):
                self.n += 1
                instruction.then_inc(self.done, 1)
                self.eng.wait_ge(self.done, self.base + self.n)

            def add(self, instruction):
                self.n += 1
                instruction.then_inc(self.done, 1)

            def end(self):
                assert self.n == self.per, (self.done, self.n)

        @block.sync
        def _(sp):
            def load(dst, src):
                sp.dma_start(dst, src).then_inc(s.weights_in, 16)
            for i, w in enumerate((wk0, wq0, wv0)):
                load(NAT[:, i, :], w)
            load(NAT[:, 3:6, :], wih.rearrange("(k p) d -> p k d", p=P))
            load(NAT[:, 6:9, :], whh.rearrange("(k p) d -> p k d", p=P))
            load(NAT[:, 9, :], w0)
            load(NAT[:, 10, :], a0.rearrange("e r d -> (e r) d"))
            load(NAT[:, 11, :].rearrange("p (e r) -> p e r", e=E), lb0.rearrange("e o r -> o e r"))
            for i, w in enumerate((wq1, wk1, wv1, wo1)):
                load(NAT[:, 12 + i, :], w)
            load(NAT[0:E, 16, :], r0)
            load(WR[:, :], wr)

            def load_group(t):
                sp.wait_ge(s.turned, 3 * t)
                sp.dma_start(x_tok[:, :, :], x[bass.ds(t * GB, GB), :, :].rearrange("b s d -> s b d")
                             ).then_inc(s.x_in, 16)
                sp.wait_ge(s.ctx_squared, t)
                sp.dma_start(ctx_tok[:, :, :], ctx[bass.ds(t * GB, GB), :, :].rearrange("b s d -> s b d")
                             ).then_inc(s.ctx_in, 16)

            loop(sp, 0, NG, load_group)
            for e in range(E):
                sp.dma_start(proj_b_all[:, e, :], bproj[e:e + 1, :].broadcast_to([P, P])).then_inc(s.experts_in, 16)
                sp.dma_start(fc_b_all[:, e * HC:(e + 1) * HC], bfc[e, :].rearrange("(p c) -> p c", c=HC)
                             ).then_inc(s.experts_in, 16)
            for dst, src in ((fcs_w[:, :], wfc_s), (fcs_b[:, :], bfc_s.rearrange("(p c) -> p c", c=HC)),
                             (projs_w[:, :, :], wproj_s.rearrange("(p c) n -> p c n", c=HC)),
                             (projs_b[:, :], bproj_s.rearrange("(a n) -> a n", a=1).broadcast_to([P, P]))):
                sp.dma_start(dst, src).then_inc(s.shared_in, 16)

            sp.wait_ge(s.x2_ready, NG)
            sp.dma_start(fc_all.rearrange("p (e h) -> p e h", e=E), wfc.rearrange("e d h -> d e h")
                         ).then_inc(s.experts_in, 16)
            sp.dma_start(proj_all.rearrange("p (e n) -> p e n", e=E), wproj.rearrange("e (p c) n -> p e (c n)", c=HC)
                         ).then_inc(s.experts_in, 16)

            def store_y(p, h, j):
                sp.wait_ge(y_ready[p], h + 1)
                sp.dma_start(y_dram[bass.ds(j * ER, ER), :].rearrange("(p c) d -> p c d", c=2), y_out[:, p, :, :]
                             ).then_inc(y_stored[p], 16)

            def tile_pair(m):
                for p in range(2):
                    store_y(p, m - 1, 2 * m - 2 + p)

            loop(sp, 1, PAIRS, tile_pair)
            store_y(0, PAIRS - 1, 2 * PAIRS - 2)
            store_y(1, PAIRS - 1, 2 * PAIRS - 1)
            store_y(0, PAIRS, 2 * PAIRS)

            sp.wait_ge(s.x3_stored, 16 * NG)
            sp.wait_ge(s.xn3_stored, 16 * NG)

            def load_c(p, h, g):
                cols = bass.ds(g * GT, GT)
                sp.wait_ge(fc_s_done[p], HC * h)
                sp.dma_start(xn3_in[:, p, :], xn3_dram[:, cols]).then_inc(c_xn3_in[p], 16)
                sp.wait_ge(sum_done[p], h)
                sp.dma_start(x3_in[:, p, :], x3_dram[:, cols]).then_inc(c_x3_in[p], 16)

            def store_out(p, h, g):
                sp.wait_ge(total_ready[p], h + 1)
                sp.dma_start(out[bass.ds(g * GB, GB), :, :].rearrange("b s d -> s b d"), total[:, p, :, :]
                             ).then_inc(out_stored[p], 16)

            load_c(0, 0, 0)
            load_c(1, 0, 1)
            def group_pair(m):
                for p in range(2):
                    load_c(p, m, 2 * m + p)
                    store_out(p, m - 1, 2 * m - 2 + p)

            loop(sp, 1, NG // 2, group_pair)
            for p in range(2):
                store_out(p, NG // 2 - 1, NG - 2 + p)
            for p in range(2):
                sp.wait_ge(out_stored[p], 16 * (NG // 2))

        @block.gpsimd
        def _(pool):
            made = [0]

            def make(instruction):
                made[0] += 1
                instruction.then_inc(s.consts_made, 1)

            def made_all():
                pool.wait_ge(s.consts_made, made[0])

            make(pool.memset(ident[:, :], 0.0))
            make(pool.memset(mean_w[:, :], 1.0 / D))
            make(pool.memset(ones[:, :], 1.0))
            make(pool.memset(quad_sel[:, :, :], 1.0))
            make(pool.memset(sum_w[:, :, :], 0.0))
            make(pool.memset(k_quad[:, :, :, :], 0.0))
            make(pool.memset(v_pad[:, :, :], 0.0))
            make(pool.memset(count[:, :], 0.0))
            make(pool.memset(power[:, :], -0.5))
            make(pool.memset(rms_eps[:, :], RMS_EPS))
            make(pool.memset(ln_eps[:, :], LN_EPS))
            make(pool.memset(prob[:, :], 0.0))
            make(pool.memset(prob_rz[:, :], 1.0))
            make(pool.memset(zeros[:, :], 0.0))
            make(pool.memset(base_of[:, :], 0.0))
            make(pool.iota(step_i[:, :], [[ER, NT // ER]], base=0, channel_multiplier=0))
            make(pool.iota(tile_i[:, :], [[1, EXPERT_TILES]], base=0, channel_multiplier=0))
            make(pool.memset(earlier[:, :, :], 1.0))
            make(pool.iota(region_i[:, :], [[1, E]], base=0, channel_multiplier=0))
            made_all()
            make(pool.affine_select(out=ident[:, :], in_=ident[:, :], compare_op=ALU.not_equal, fill=1.0,
                                    base=0, pattern=[[-1, P]], channel_multiplier=1))
            make(pool.affine_select(out=before[:, :], in_=ones[:, :], compare_op=ALU.is_gt, fill=0.0,
                                    base=0, pattern=[[1, P]], channel_multiplier=-1))
            make(pool.affine_select(out=quad_sel[:, :, :], in_=quad_sel[:, :, :], compare_op=ALU.is_ge, fill=0.0,
                                    base=0, pattern=[[-DK, 4], [-32, Q]], channel_multiplier=1))
            make(pool.affine_select(out=prob[:, :], in_=prob[:, :], compare_op=ALU.not_equal, fill=RMS_EPS,
                                    base=-M, pattern=[[0, GT]], channel_multiplier=1))
            for u in range(4):
                make(pool.memset(sum_w[:, u, DK * u:DK * u + DK], 1.0))
            make(pool.affine_select(out=earlier[:, :, :], in_=earlier[:, :, :], compare_op=ALU.is_gt, fill=0.0,
                                    base=0, pattern=[[1, E], [-1, E]], channel_multiplier=0))
            make(pool.tensor_copy(step_at[:, :], step_i[:, :]))
            make(pool.tensor_copy(tile_no[:, :], tile_i[:, :]))
            made_all()
            make(pool.affine_select(out=quad_sel[:, :, :], in_=quad_sel[:, :, :], compare_op=ALU.is_ge, fill=0.0,
                                    base=DK - 1, pattern=[[DK, 4], [32, Q]], channel_multiplier=-1))
            make(pool.tensor_scalar(center_w[:, :], ident[:, :], 1.0 / D, None, ALU.subtract))
            make(pool.tensor_scalar(region_at[:, :], region_i[:, :], float(REGION), None, ALU.mult))
            assert made[0] == CONSTS
            for i, v in ((IH, bih), (HH, bhh)):
                pool.dma_start(vec_rows[i:i + 3, :], v.rearrange("(k p) -> k p", p=P)).then_inc(s.columns_in, 16)
            for i, v in ((SLOT_W, slot_w), (IN_W, in_w), (B0, b0), (BQ, bq1), (BK, bk1), (BV, bv1), (BO1, bo1)):
                pool.dma_start(vec_rows[i:i + 1, :], v.rearrange("(k p) -> k p", k=1)).then_inc(s.columns_in, 16)

            def slots_step(t, step, i=0):
                if step == "stats":
                    pool.wait_ge(s.var_ready, t + 1)
                    pool.tensor_tensor(rs_tok[:, :], var_tok[:, :], power[:, :], ALU.pow).then_inc(s.roots_ready, 1)
                if step == "context_stats":
                    pool.wait_ge(s.ctx_in, 16 * t + 16)
                    pool.wait_ge(s.ctx_scale, t)
                    pool.tensor_tensor(ctx_sq[:, :, :], ctx_tok[:, :, :], ctx_tok[:, :, :], ALU.mult
                                       ).then_inc(s.ctx_squared, 1)
                    pool.wait_ge(s.ctx_ms_ready, t + 1)
                    pool.tensor_tensor(ctx_r[:, :], ctx_ms[:, :], power[0:M, :], ALU.pow).then_inc(s.roots_ready, 1)
                if step == "cell":
                    wait_apart(pool, (s.z_tanh_ready, 3 * t + i + 1))
                    pool.tensor_scalar(z_gate[:, :], z_tanh[:, :], 0.5, 0.5, ALU.mult, ALU.add
                                       ).then_inc(s.z_gate_ready, 1)
                    pool.wait_ge(s.z_gate_ready, 3 * t + i + 1)
                    pool.tensor_tensor(kept[:, :], z_gate[:, :], slots[:, :], ALU.mult).then_inc(s.kept_ready, 1)

            def heads_step(a, step, k=0):
                if step == "center":
                    wait_apart(pool, (s.x3_ready, a + 1))
                    pool.dma_start(x3_dram[:, bass.ds(a * GT, GT)], x3[:, :]).then_inc(s.x3_stored, 16)
                if step == "rank":
                    wait_apart(pool, (s.xn3_ready, a + 1))
                    pool.dma_start(xn3_dram[:, bass.ds(a * GT, GT)], xn3[:, :]).then_inc(s.xn3_stored, 16)
                    wait_apart(pool, (s.xn3_tok_ready, a + 1), (s.scatter_ready, a + 1))
                    for c in range(2):
                        for b in range(GB):
                            pool.indirect_dma_start(
                                rows_dram, bass.IndirectOffsetOnAxis(ap=scatter_at[:, c, b:b + 1], axis=0),
                                xn3_tok[:, b, :], None).then_inc(s.scattered, 16)

            groups(pool, slots_step, heads_step)
            pool.wait_ge(s.pad_ready, 1)
            for e in range(E):
                row = pool.value_load(pad_at[0:1, e:e + 1], min_val=0, max_val=E * REGION - ER)
                pool.dma_start(rows_dram[bass.ds(row, ER), :].rearrange("(p c) d -> p c d", c=2),
                               zeros[:, :].unsqueeze(1).broadcast_to([P, 2, P])).then_inc(s.scattered, 16)
            pool.wait_ge(s.scattered, 128 * NG + 16 * E)
            pool.wait_ge(s.table_ready, 1)

            def load_rows(p, h, j):
                row = pool.value_load(table[0:1, 0, bass.ds(j, 1)], min_val=0, max_val=E * REGION - ER)
                wait_apart(pool, (rows_turned[p], h))
                pool.dma_start(rows[:, p, :, :], rows_dram[bass.ds(row, ER), :].rearrange("(p c) d -> p c d", c=2)
                               ).then_inc(rows_in[p], 16)

            def tile_pair(m):
                for p in range(2):
                    load_rows(p, m, 2 * m + p)

            loop(pool, 0, PAIRS, tile_pair)
            load_rows(0, PAIRS, 2 * PAIRS)

            pool.wait_ge(s.place_ready, 1)
            pool.wait_ge(y_stored[0], 16 * (PAIRS + 1))
            pool.wait_ge(y_stored[1], 16 * PAIRS)

            def gather(p, h, g):
                pool.wait_ge(total_ready[p], h)
                pool.tensor_copy(y_now[:, p, :, :], y_at[:, :, bass.ds(g * GB, GB)]).then_inc(s.y_now_ready, 1)
                wait_apart(pool, (s.y_now_ready, g + 1))
                for c in range(2):
                    for b in range(GB):
                        pool.indirect_dma_start(y_in[:, p, c, b, :], None, y_dram,
                                                bass.IndirectOffsetOnAxis(ap=y_now[:, p, c, b:b + 1], axis=0)
                                                ).then_inc(y_gathered[p], 16)

            def group_pair(m):
                for p in range(2):
                    gather(p, m, 2 * m + p)

            loop(pool, 0, NG // 2, group_pair)

        @block.scalar
        def _(act):
            def copy(dst, src, scale=1.0):
                return act.activation(dst, src, ACT.Copy, scale=scale)

            def inverse_root(ln, dst, src, eps, ln_signal, signal, n):
                act.activation(ln, src, ACT.Ln, bias=eps).then_inc(ln_signal, 1)
                act.wait_ge(ln_signal, n + 1)
                act.activation(dst, ln, ACT.Exp, scale=-0.5).then_inc(signal, 1)

            act.preload_act_table_set(LN_SET)
            act.wait_ge(s.consts_made, CONSTS)
            act.wait_ge(s.turned_w, 5)
            copy(TW[:, 0:4, :], bank[0][:, :]).then_inc(s.turned_w_out, 1)
            copy(TW[:, 4:8, :], bank[1][:, :]).then_inc(s.turned_w_out, 1)

            def slots_step(t, step, i=0):
                n = 3 * t + i
                if step == "turn":
                    act.wait_ge(s.turned, 3 * t + 1)
                    act.activation(slot_sq[:, :], G3[:, :], ACT.Square).then_inc(s.squared, 1)
                    copy(slots[:, :], G3[:, :]).then_inc(s.slots_in, 1)
                    act.wait_ge(s.turned, 3 * t + 3)
                    copy(xT[:, :], G2[:, :]).then_inc(s.xT_ready, 1)
                if step == "keys":
                    act.wait_ge(s.ctx_scale, t + 1)
                    for b, src in ((0, G0), (1, G2)):
                        act.wait_ge(s.values_done, 4 * t + b + 1)
                        copy(values[:, b, :], src[0:M, 0:3 * P], ctx_r[:, b:b + 1]).then_inc(s.values_by_act, 1)
                if step == "score":
                    if i > 0:
                        act.wait_ge(s.slots_new, n)
                        act.activation(slot_sq[:, :], slots[:, :], ACT.Square).then_inc(s.squared, 1)
                    act.wait_ge(s.sumsq_done, n + 1)
                    inverse_root(slot_ln[:, :], slot_r[:, :], G1[0:M, :], rms_eps[0:M, :], s.slot_ln, s.slot_r_ready, n)
                if step == "probs":
                    act.wait_ge(s.bias_ready, n + 1)
                    for b in range(GB):
                        c = slice(b * P, (b + 1) * P)
                        last = act.activation(prob[0:M, c], score[:, c], ACT.Exp, bias=score_b[:, b:b + 1],
                                              scale=ctx_sc[:, b:b + 1], accum_out=prob_sum[:, b:b + 1])
                    last.then_inc(s.exp_done, 1)
                if step == "share_sum":
                    act.wait_ge(s.share_summed, n + 1)
                    act.activation(slot_ln[:, :], G0[0:M, :], ACT.Ln).then_inc(s.share_ln, 1)
                    act.wait_ge(s.share_ln, n + 1)
                    act.activation(share_rz[:, :], slot_ln[:, :], ACT.Exp, scale=-1.0).then_inc(s.share_rz_ready, 1)
                    act.preload_act_table_set(TANH_SET)
                if step == "hidden":
                    act.wait_ge(s.hn_done, n + 1)
                    act.activation(hn[:, :], G2[:, :], ACT.Identity, bias=col[:, HH + 2:HH + 3]
                                   ).then_inc(s.hn_biased, 1)
                if step == "gates":
                    act.wait_ge(s.r_done, n + 1)
                    act.activation(r_tanh[:, :], G3[:, :], ACT.Tanh, bias=half_b[:, 0:1], scale=0.5
                                   ).then_inc(s.r_tanh_ready, 1)
                    act.wait_ge(s.z_done, n + 1)
                    act.activation(z_tanh[:, :], G1[:, :], ACT.Tanh, bias=half_b[:, 1:2], scale=0.5
                                   ).then_inc(s.z_tanh_ready, 1)
                if step == "cell":
                    act.wait_ge(s.cell_ready, n + 1)
                    act.activation(n_new[:, :], n_pre[:, :], ACT.Tanh, bias=col[:, IH + 2:IH + 3]
                                   ).then_inc(s.n_ready, 1)
                    act.preload_act_table_set(LN_SET)
                if step == "center":
                    act.wait_ge(s.c1_done, t + 1)
                    act.activation(c1_sq[:, :], G0[:, :], ACT.Square).then_inc(s.c1_squared, 1)
                if step == "spread":
                    act.wait_ge(s.v1_done, t + 1)
                    inverse_root(ln_buf[:, 0, :], rs1[:, :], G1[:, :], ln_eps[:, :], s.v1_ln, s.rs1_ready, t)
                if step == "route":
                    act.wait_ge(s.gate_shifted, t + 1)
                    act.activation(top["e"][:, :, :], top["low"][:, :, :], ACT.Exp).then_inc(s.gate_exp, 1)
                if step == "turn_gate":
                    act.wait_ge(s.gate_turned, t + 1)
                    copy(gate_T[:, :], G0[:, :]).then_inc(s.gate_T_ready, 1)

            def heads_step(a, step, k=0):
                n = UNITS * a + k
                if step == "keys":
                    act.wait_ge(s.v_done, a + 1)
                    copy(v_pad[:, :, :].rearrange("m c (u w) -> m c u w", u=4)[:, :, :, 0:DK],
                         BO[0:M, :].rearrange("m (c u d) -> m c u d", u=4, d=DK)).then_inc(s.v_ready, 1)
                if step == "norm":
                    act.wait_ge(s.c2_done, a + 1)
                    act.activation(c2_sq[:, :], BO[:, :], ACT.Square).then_inc(s.c2_squared, 1)
                if step == "norm_spread":
                    act.wait_ge(s.rs3_ready, a)
                    act.wait_ge(s.v2_done, a + 1)
                    inverse_root(ln_buf[:, 1, :], rs2[:, :], BT[:, :], ln_eps[:, :], s.v2_ln, s.rs2_ready, a)
                if step == "project":
                    act.wait_ge(s.q_done, a + 1)
                    for u in (0, 1):
                        act.activation(q_mask[:, u, :], BS[:, :], ACT.Identity, bias=bq_mask[:, u:u + 1],
                                       scale=quad_mask[:, u:u + 1]).then_inc(s.q_by_act, 1)
                if step == "unit_score":
                    act.wait_ge(s.head_shifted, n + 1)
                    act.wait_ge(s.head_turned, n - 1 if k >= 2 else UNITS * a)
                    act.activation(head_p[:, k % 2, :, :], head_s[:, k % 2, :, :], ACT.Exp, scale=HSCALE
                                   ).then_inc(s.head_exp, 1)
                if step == "unit_turn":
                    act.wait_ge(s.head_turned, n + 1)
                    act.wait_ge(s.head_summed, n - 1 if k >= 2 else UNITS * a)
                    copy(head_pT[:, k % 2, :], BT[0:M, :]).then_inc(s.head_pT_ready, 1)
                if step == "mix":
                    act.wait_ge(s.head_summed, UNITS * (a + 1))
                    act.activation(ln_buf[:, 1, :], BZ[:, :], ACT.Ln).then_inc(s.o_ln, 1)
                    act.wait_ge(s.o_ln, a + 1)
                    act.activation(o_rz[:, :], ln_buf[:, 1, :], ACT.Exp, scale=-1.0).then_inc(s.o_rz_ready, 1)
                if step == "center":
                    act.wait_ge(s.c3_done, a + 1)
                    act.activation(c3_sq[:, :], BS[:, :], ACT.Square).then_inc(s.c3_squared, 1)
                if step == "spread":
                    act.wait_ge(s.v3_done, a + 1)
                    inverse_root(ln_buf[:, 1, :], rs3[:, :], BZ[:, :], ln_eps[:, :], s.v3_ln, s.rs3_ready, a)
                if step == "route":
                    act.wait_ge(s.xn3_turned, a + 1)
                    act.wait_ge(s.scattered, 128 * a)
                    copy(xn3_tok[:, :, :], BS[:, :]).then_inc(s.xn3_tok_ready, 1)
                    act.wait_ge(s.gap_ready, a + 1)
                    act.activation(mo1["e"][:, :], mo1["d"][:, :], ACT.Exp).then_inc(s.gap_exp, 1)

            groups(act, slots_step, heads_step)

            act.wait_ge(s.table_ready, 1)
            act.wait_ge(s.experts_in, EXPERT_LOADS)

            def take_proj_w(p, h, j):
                e = act.value_load(table[0:1, 1, bass.ds(j, 1)], min_val=0, max_val=E - 1)
                act.wait_ge(proj_done[p], h)
                act.activation(proj_w[:, p, :], proj_all[:, bass.ds(e * (HC * P), HC * P)], ACT.Copy
                               ).then_inc(proj_w_in[p], 1)

            def gelu(p, h):
                act.wait_ge(fc_w_in[p], h + 1)
                act.wait_ge(proj_done[p], h)
                act.wait_ge(fc_done[p], h + 1)
                for c in range(HC):
                    last = act.activation(hidden[:, p, c, :], FC[p][c // 2][:, (c % 2) * ER:(c % 2 + 1) * ER],
                                          ACT.Gelu_apprx_tanh, bias=fc_b[:, p, c:c + 1])
                last.then_inc(gelu_done[p], 1)

            def tile_pair(m):
                for p in range(2):
                    take_proj_w(p, m, 2 * m + p)
                    gelu(p, m)

            loop(act, 0, PAIRS, tile_pair)
            take_proj_w(0, PAIRS, 2 * PAIRS)
            gelu(0, PAIRS)

            act.wait_ge(s.shared_in, 64)

            def gelu_shared(p, h):
                act.wait_ge(sum_done[p], h)
                for c in range(HC):
                    act.wait_ge(fc_s_done[p], HC * h + c + 1)
                    act.activation(hidden_s[:, p, c, :], bank[c][:, :], ACT.Gelu_apprx_tanh, bias=fcs_b[:, c:c + 1]
                                   ).then_inc(gelu_s_done[p], 1)

            def group_pair(m):
                for p in range(2):
                    gelu_shared(p, m)

            loop(act, 0, NG // 2, group_pair)

        @block.vector
        def _(dve):
            dve.wait_ge(s.consts_made, CONSTS)
            setup = Chain(dve, s.weights_ready, 11)
            setup.start(0)
            setup(dve.reduce_sum(quad_mask[:, :], quad_sel[:, :, :], AX_X))
            dve.wait_ge(s.turned_w, 1)
            setup(dve.tensor_copy(col[:, :], bank[7][:, 0:13]))
            setup(dve.tensor_tensor(half_b[:, :], col[:, IH:IH + 2], col[:, HH:HH + 2], ALU.add))
            setup(dve.tensor_scalar(half_b[:, :], half_b[:, :], 0.5, None, ALU.mult))
            setup(dve.tensor_scalar(bq_mask[:, :], quad_mask[:, :], col[:, BQ:BQ + 1], None, ALU.mult))
            dve.wait_ge(s.turned_w, 5)
            setup(dve.tensor_copy(TW[:, 8:12, :], bank[2][:, :]))
            setup(dve.tensor_copy(TW[:, 12, :], bank[3][:, 0:P]))
            setup(dve.tensor_copy(RT[:, :], bank[3][:, P:P + E]))
            dve.wait_ge(s.fused_w, 3)
            setup(dve.tensor_scalar(KQ_W[:, :], bank[4][:, 0:P], col[:, IN_W:IN_W + 1], None, ALU.mult))
            setup(dve.tensor_scalar(VG_W[:, :], bank[5][:, 0:3 * P], col[:, IN_W:IN_W + 1], None, ALU.mult))
            setup(dve.tensor_tensor(bo_all[:, :], bank[6][:, 0:1], col[:, BO1:BO1 + 1], ALU.add))
            setup.end()

            slots_link = Chain(dve, s.slots_chain, SLOTS_LINKS)
            heads_link = Chain(dve, s.heads_chain, HEADS_LINKS)
            tail_link = Chain(dve, s.tail_chain, TAIL_LINKS)
            early = Chain(dve, s.stats_chain, 2)

            every_two = [P, GB, E, E]

            def places(link, logits, w, vs):
                link(dve.tensor_copy(w["logits"][:, :, :], logits))
                ones_l = w["logits"][:, :, :].unsqueeze(3).broadcast_to(every_two)
                others_l = w["logits"][:, :, :].unsqueeze(2).broadcast_to(every_two)
                link.add(dve.tensor_tensor(vs["above"][:, :, :, :], others_l, ones_l, ALU.is_gt))
                link(dve.tensor_tensor(vs["equal"][:, :, :, :], others_l, ones_l, ALU.is_equal))
                link(dve.tensor_tensor(vs["equal"][:, :, :, :], vs["equal"][:, :, :, :],
                                       earlier[:, :, :].unsqueeze(1).broadcast_to(every_two), ALU.mult))
                link(dve.tensor_tensor(vs["above"][:, :, :, :], vs["above"][:, :, :, :], vs["equal"][:, :, :, :],
                                       ALU.add))
                link(dve.reduce_sum(w["place"][:, :, :], vs["above"][:, :, :, :], AX_X))

            def slots_step(t, step, i=0):
                link = slots_link
                n = 3 * t + i
                if step == "stats":
                    early.start(t)
                    dve.wait_ge(s.x_in, 16 * t + 16)
                    for b in range(GB):
                        last = dve.bn_stats(stats[:, b, :], x_tok[:, b, :])
                    last.then_inc(s.stats_ready, 1)
                    wait_apart(dve, (s.stats_ready, t + 1))
                    for b in range(GB):
                        last = dve.bn_aggr(mv[:, b, :], stats[:, b, :])
                    early(last)
                    dve.tensor_scalar(var_tok[:, :], mv[:, :, 1], LN_EPS, None, ALU.add).then_inc(s.var_ready, 1)
                if step == "normal":
                    dve.wait_ge(s.roots_ready, 2 * t + 1)
                    for b in range(GB):
                        last = dve.tensor_scalar(xln[:, b, :], x_tok[:, b, :], mv[:, b, 0:1], rs_tok[:, b:b + 1],
                                                 ALU.subtract, ALU.mult)
                    last.then_inc(s.xln_ready, 1)
                if step == "context_stats":
                    dve.wait_ge(s.ctx_squared, t + 1)
                    early(dve.reduce_sum(ctx_ms[:, :], ctx_sq[:, :, :], AX_X))
                    dve.tensor_scalar(ctx_ms[:, :], ctx_ms[:, :], 1.0 / D, RMS_EPS, ALU.mult, ALU.add
                                      ).then_inc(s.ctx_ms_ready, 1)
                    dve.wait_ge(s.roots_ready, 2 * t + 2)
                    dve.tensor_scalar(ctx_sc[:, :], ctx_r[:, :], SCALE, None, ALU.mult)
                    dve.tensor_scalar(ctx_nsc[:, :], ctx_r[:, :], -SCALE, None, ALU.mult).then_inc(s.ctx_scale, 1)
                    early.end()
                if step == "turn":
                    link.start(t)
                    dve.wait_ge(s.turned, 3 * t + 2)
                    dve.wait_ge(s.v_done, t)
                    dve.tensor_copy(ctxT[:, :], G0[:, 0:CM]).then_inc(s.ctxT_ready, 1)
                if step == "keys":
                    dve.wait_ge(s.keys_done, t + 1)
                    dve.tensor_scalar(keysT[:, :], G1[:, 0:CM], col[:, SLOT_W:SLOT_W + 1], None, ALU.mult
                                      ).then_inc(s.keys_ready, 1)
                    dve.wait_ge(s.ctx_scale, t + 1)
                    for b, src in ((2, G3), (3, G1)):
                        dve.wait_ge(s.values_done, 4 * t + b + 1)
                        dve.tensor_scalar(values[:, b, :], src[0:M, 0:3 * P], ctx_r[:, b:b + 1], None, ALU.mult
                                          ).then_inc(s.values_by_dve, 1)
                if step == "score":
                    dve.wait_ge(s.slot_r_ready, n + 1)
                    dve.wait_ge(s.scored, n + 1)
                    dve.tensor_tensor(score[:, :], G0[0:M, :], slot_r[:, :], ALU.mult).then_inc(s.score_read, 1)
                    dve.wait_ge(s.score_read, n + 1)
                    link(dve.reduce_max(score_max[:, :], score[:, :].rearrange("m (b k) -> m b k", b=GB), AX_X))
                    dve.tensor_tensor(score_b[:, :], score_max[:, :], ctx_nsc[:, :], ALU.mult
                                      ).then_inc(s.bias_ready, 1)
                if step == "probs":
                    dve.wait_ge(s.exp_done, n + 1)
                    dve.reciprocal(prob_rz[0:M, :], prob_sum[:, :]).then_inc(s.rz_ready, 1)
                    dve.wait_ge(s.rz_ready, n + 1)
                    for b in range(GB):
                        c = slice(b * P, (b + 1) * P)
                        last = dve.tensor_scalar(prob_n[:, c], prob[0:M, c], prob_rz[0:M, b:b + 1], None, ALU.mult)
                    link(last)
                if step == "share":
                    dve.wait_ge(s.share_rz_ready, n + 1)
                    dve.tensor_tensor(share[:, :], prob_n[:, :], share_rz[:, :], ALU.mult).then_inc(s.share_ready, 1)
                if step == "cell":
                    dve.wait_ge(s.hn_biased, n + 1)
                    dve.wait_ge(s.r_tanh_ready, n + 1)
                    link(dve.scalar_tensor_tensor(hn_part[:, :], r_tanh[:, :], 1.0, hn[:, :], ALU.add, ALU.mult))
                    dve.wait_ge(s.xn_done, n + 1)
                    dve.scalar_tensor_tensor(n_pre[:, :], hn_part[:, :], 0.5, G0[:, :], ALU.mult, ALU.add
                                             ).then_inc(s.cell_ready, 1)
                    dve.wait_ge(s.z_tanh_ready, n + 1)
                    link(dve.tensor_scalar(n_share[:, :], z_tanh[:, :], -0.5, 0.5, ALU.mult, ALU.add))
                if step == "update":
                    dve.wait_ge(s.n_ready, n + 1)
                    link(dve.tensor_tensor(n_taken[:, :], n_share[:, :], n_new[:, :], ALU.mult))
                    dve.wait_ge(s.kept_ready, n + 1)
                    dve.tensor_tensor(slots[:, :], n_taken[:, :], kept[:, :], ALU.add).then_inc(s.slots_new, 1)
                if step == "center":
                    dve.wait_ge(s.slots_new, 3 * t + 3)
                    dve.wait_ge(s.xT_ready, t + 1)
                    dve.tensor_tensor(x1[:, :], xT[:, :], slots[:, :], ALU.add).then_inc(s.x1_ready, 1)
                if step == "spread":
                    dve.wait_ge(s.rs1_ready, t + 1)
                    dve.tensor_tensor(xn1[:, :], G0[:, :], rs1[:, :], ALU.mult).then_inc(s.xn1_ready, 1)
                if step == "route":
                    dve.wait_ge(s.logits1_done, t + 1)
                    logits = G2[:, 0:GB * E].rearrange("p (b e) -> p b e", b=GB)
                    spread = lambda v: v.unsqueeze(2).broadcast_to([P, GB, E])
                    link(dve.reduce_max(top1["max"][:, :], logits, AX_X))
                    dve.tensor_tensor(top["low"][:, :, :], logits, spread(top1["max"][:, :]), ALU.subtract
                                      ).then_inc(s.gate_shifted, 1)
                    places(link, logits, top, top_vs)
                if step == "gate":
                    spread = lambda v: v.unsqueeze(2).broadcast_to([P, GB, E])
                    dve.wait_ge(s.gate_exp, t + 1)
                    link.add(dve.reduce_sum(top1["z"][:, :], top["e"][:, :, :], AX_X))
                    link(dve.scalar_tensor_tensor(top["both"][:, :, :], top["place"][:, :, :], 2.0, top["e"][:, :, :],
                                                  ALU.is_lt, ALU.mult))
                    link(dve.reduce_sum(top1["s"][:, :], top["both"][:, :, :], AX_X))
                    link(dve.scalar_tensor_tensor(top1["g"][:, :], top1["z"][:, :], RMS_EPS, top1["s"][:, :],
                                                  ALU.mult, ALU.add))
                    link(dve.reciprocal(top1["g"][:, :], top1["g"][:, :]))
                    link(dve.tensor_tensor(top["both"][:, :, :], top["both"][:, :, :], spread(top1["g"][:, :]),
                                           ALU.mult))
                    dve.tensor_copy(gate_x[:, :, :, :],
                                    top["both"][:, :, :].unsqueeze(3).broadcast_to([P, GB, E, R])
                                    ).then_inc(s.gate_ready, 1)
                if step == "turn_gate":
                    dve.wait_ge(s.gate_T_ready, t + 1)
                    dve.wait_ge(s.down_done, t + 1)
                    dve.tensor_tensor(down[:, :], G3[:, :], gate_T[:, :], ALU.mult).then_inc(s.down_ready, 1)
                if step == "out":
                    dve.wait_ge(s.ffn1_done, t + 1)
                    dve.wait_ge(s.x3_ready, t)
                    dve.scalar_tensor_tensor(x2[:, :], G1[:, :], col[:, B0:B0 + 1], x1[:, :], ALU.add, ALU.add
                                             ).then_inc(s.x2_ready, 1)
                    link.end()

            def heads_step(a, step, k=0):
                link = heads_link
                n = UNITS * a + k
                if step == "keys_out":
                    dve.wait_ge(s.k_done, a + 1)
                    for g in range(Q):
                        rows = slice(32 * g, 32 * g + 32)
                        last = dve.tensor_scalar(k_quad[rows, :, g, :],
                                                 BT[rows, 0:CM].rearrange("p (b m) -> p b m", b=GB),
                                                 col[rows, BK:BK + 1], None, ALU.add)
                    last.then_inc(s.k_ready, 1)
                if step == "norm_spread":
                    link.start(a)
                    dve.wait_ge(s.rs2_ready, a + 1)
                    dve.tensor_tensor(xn2[:, :], BO[:, :], rs2[:, :], ALU.mult).then_inc(s.xn2_ready, 1)
                if step == "project":
                    dve.wait_ge(s.q_by_act, 2 * a + 2)
                    for u in (2, 3):
                        dve.tensor_scalar(q_mask[:, u, :], BS[:, :], col[:, BQ:BQ + 1], quad_mask[:, u:u + 1],
                                          ALU.add, ALU.mult).then_inc(s.q_by_dve, 1)
                if step == "unit_score":
                    dve.wait_ge(s.head_scored, n + 1)
                    sc = BS[:, 0:Q * M].rearrange("p (g m) -> p g m", g=Q)
                    link(dve.reduce_max(head_max[:, k % 2, :], sc, AX_X))
                    if k >= 2:
                        dve.wait_ge(s.head_exp, n - 1)
                    else:
                        dve.wait_ge(s.head_exp, UNITS * a)
                    dve.tensor_tensor(head_s[:, k % 2, :, :], sc,
                                      head_max[:, k % 2, :].unsqueeze(2).broadcast_to([P, Q, M]), ALU.subtract
                                      ).then_inc(s.head_shifted, 1)
                if step == "mix":
                    dve.wait_ge(s.o_rz_ready, a + 1)
                    dve.tensor_tensor(o_all[:, :], BO[:, :], o_rz[:, :], ALU.mult).then_inc(s.attended, 1)
                if step == "residual":
                    link.end()
                    dve.wait_ge(s.wo_done, a + 1)
                    dve.wait_ge(s.x3_stored, 16 * a)
                    dve.scalar_tensor_tensor(x3[:, :], BS[:, :], bo_all[:, 0:1], x2[:, :], ALU.add, ALU.add
                                             ).then_inc(s.x3_ready, 1)
                if step == "spread":
                    dve.wait_ge(s.rs3_ready, a + 1)
                    dve.wait_ge(s.xn3_stored, 16 * a)
                    dve.tensor_tensor(xn3[:, :], BS[:, :], rs3[:, :], ALU.mult).then_inc(s.xn3_ready, 1)
                if step == "route":
                    tail_link.start(a)
                    dve.wait_ge(s.logits2_done, a + 1)
                    logits = BZ[:, 0:GB * E].rearrange("p (b e) -> p b e", b=GB)
                    places(tail_link, logits, mo, mo_vs)
                    dve.tensor_scalar(mo["both"][:, :, :], mo["place"][:, :, :], 2.0, None, ALU.is_lt
                                      ).then_inc(s.both_ready, 1)
                    for c in range(2):
                        last = dve.tensor_scalar(mo2["pick"][:, c, :, :], mo["place"][:, :, :], float(c), None,
                                                 ALU.is_equal)
                    tail_link(last)
                    tail_link(dve.tensor_tensor(mo["sign"][:, :, :], mo2["pick"][:, 1, :, :], mo2["pick"][:, 0, :, :],
                                           ALU.subtract))
                    tail_link(dve.tensor_tensor(mo["sign"][:, :, :], mo["sign"][:, :, :], mo["logits"][:, :, :], ALU.mult))
                    dve.reduce_sum(mo1["d"][:, :], mo["sign"][:, :, :], AX_X).then_inc(s.gap_ready, 1)
                    dve.tensor_copy(pick_of[:, :, bass.ds(a * GB, GB), :], mo2["pick"][:, :, :, :])
                if step == "rank":
                    tiles = bass.ds(a * GB, GB)
                    dve.wait_ge(s.gap_exp, a + 1)
                    tail_link(dve.tensor_scalar(mo1["s"][:, :], mo1["e"][:, :], 1.0, None, ALU.add))
                    tail_link(dve.reciprocal(mo1["s"][:, :], mo1["s"][:, :]))
                    dve.tensor_copy(gate_of[:, 0, tiles], mo1["s"][:, :])
                    dve.tensor_tensor(gate_of[:, 1, tiles], mo1["s"][:, :], mo1["e"][:, :], ALU.mult)
                    dve.wait_ge(s.ranks_done, a + 1)
                    for b in range(GB):
                        dve.tensor_tensor(mo["rank"][:, b, :], BZ[:, (GB + b) * E:(GB + b + 1) * E], count[:, :], ALU.add)
                        tail_link(dve.tensor_tensor(count[:, :], BZ[:, (2 * GB + b) * E:(2 * GB + b + 1) * E], count[:, :], ALU.add))
                    tail_link(dve.tensor_tensor(mo["at"][:, :, :], mo["rank"][:, :, :],
                                           region_at[:, :].unsqueeze(1).broadcast_to([P, GB, E]), ALU.add))
                    both_picks = [P, 2, GB, E]
                    tail_link.add(dve.tensor_tensor(mo2["at"][:, :, :, :], mo2["pick"][:, :, :, :],
                                               mo["at"][:, :, :].unsqueeze(1).broadcast_to(both_picks), ALU.mult))
                    tail_link(dve.tensor_tensor(mo2["rank"][:, :, :, :], mo2["pick"][:, :, :, :],
                                           mo["rank"][:, :, :].unsqueeze(1).broadcast_to(both_picks), ALU.mult))
                    tail_link(dve.reduce_sum(scatter_f[:, :, :], mo2["at"][:, :, :, :], AX_X))
                    dve.wait_ge(s.scattered, 128 * a)
                    dve.tensor_copy(scatter_at[:, :, :], scatter_f[:, :, :]).then_inc(s.scatter_ready, 1)
                    dve.reduce_sum(rank_of[:, :, tiles], mo2["rank"][:, :, :, :], AX_X)
                    tail_link.end()

            groups(dve, slots_step, heads_step)

            link = Chain(dve, s.table_chain, TABLE_LINKS)
            link.start(0)
            dve.tensor_tensor(pad_at[:, :], region_at[:, :], count[:, :], ALU.add).then_inc(s.pad_ready, 1)
            steps = NT // ER
            link(dve.tensor_tensor(used[:, :, :], count[:, :].unsqueeze(2).broadcast_to([P, E, steps]),
                                   step_at[:, :].unsqueeze(1).broadcast_to([P, E, steps]), ALU.is_gt))
            link(dve.reduce_sum(tiles_of[:, :], used[:, :, :], AX_X))
            for e in range(E):
                link(dve.tensor_tensor(base_of[:, e + 1:e + 2], base_of[:, e:e + 1], tiles_of[:, e:e + 1], ALU.add))
            every = [P, EXPERT_TILES, E]
            link(dve.tensor_tensor(past[:, :, :], tile_no[:, :].unsqueeze(2).broadcast_to(every),
                                   base_of[:, 1:E + 1].unsqueeze(1).broadcast_to(every), ALU.is_ge))
            link(dve.reduce_sum(tile_e[:, :], past[:, :, :], AX_X))
            link(dve.tensor_tensor(past_w[:, :, :], past[:, :, :], tiles_of[:, :].unsqueeze(1).broadcast_to(every),
                                   ALU.mult))
            link(dve.reduce_sum(tile_b[:, :], past_w[:, :, :], AX_X))
            link(dve.tensor_scalar(tile_real[:, :], tile_e[:, :], float(E), float(ER), ALU.is_lt, ALU.mult))
            link(dve.tensor_scalar(tile_e[:, :], tile_e[:, :], float(E - 1), None, ALU.min))
            link(dve.tensor_tensor(tile_row[:, :], tile_no[:, :], tile_b[:, :], ALU.subtract))
            link(dve.tensor_tensor(tile_row[:, :], tile_row[:, :], tile_real[:, :], ALU.mult))
            link(dve.scalar_tensor_tensor(tile_row[:, :], tile_e[:, :], float(REGION), tile_row[:, :],
                                          ALU.mult, ALU.add))
            dve.tensor_copy(table[:, 1, :], tile_e[:, :])
            dve.tensor_copy(table[:, 0, :], tile_row[:, :]).then_inc(s.table_ready, 1)
            link(dve.tensor_scalar(base_rows[:, :], base_of[:, 0:E], float(ER), None, ALU.mult))
            for c in range(2):
                link(dve.tensor_tensor(place_w[:, c, :, :], pick_of[:, c, :, :],
                                       base_rows[:, :].unsqueeze(1).broadcast_to([P, TILES, E]), ALU.mult))
                link(dve.reduce_sum(place_f[:, c, :], place_w[:, c, :, :], AX_X))
            link(dve.tensor_tensor(place_f[:, :, :], place_f[:, :, :], rank_of[:, :, :], ALU.add))
            dve.tensor_copy(y_at[:, :, :], place_f[:, :, :]).then_inc(s.place_ready, 1)
            link.end()

            dve.wait_ge(s.experts_in, EXPERT_LOADS)

            def take_fc_w(p, h, j):
                e = dve.value_load(table[0:1, 1, bass.ds(j, 1)], min_val=0, max_val=E - 1)
                dve.wait_ge(fc_done[p], h)
                dve.wait_ge(gelu_done[p], h)
                dve.tensor_copy(fc_b[:, p, :], fc_b_all[:, bass.ds(e * HC, HC)])
                dve.tensor_copy(fc_w[:, p, :], fc_all[:, bass.ds(e * HID, HID)]).then_inc(fc_w_in[p], 1)

            def turn_out(p, h):
                dve.wait_ge(rows_turned[p], h + 1)
                dve.wait_ge(fc_done[p], h)
                dve.tensor_copy(rowsT[:, p, :], ROWS[p][:, 0:ER]).then_inc(rowsT_ready[p], 1)

            def y_add(p, h, j):
                e = dve.value_load(table[0:1, 1, bass.ds(j, 1)], min_val=0, max_val=E - 1)
                dve.wait_ge(proj_done[p], h + 1)
                dve.wait_ge(y_stored[p], 16 * h)
                dve.tensor_tensor(y_out[:, p, :, :], YP[p][:, 0:2 * P].rearrange("p (c d) -> p c d", c=2),
                                  proj_b_all[:, bass.ds(e, 1), :].broadcast_to([P, 2, P]), ALU.add
                                  ).then_inc(y_ready[p], 1)

            for p in range(2):
                take_fc_w(p, 0, p)
                turn_out(p, 0)

            def tile_pair(m):
                for p in range(2):
                    take_fc_w(p, m, 2 * m + p)
                    turn_out(p, m)
                    y_add(p, m - 1, 2 * m - 2 + p)

            loop(dve, 1, PAIRS, tile_pair)
            take_fc_w(0, PAIRS, 2 * PAIRS)
            turn_out(0, PAIRS)
            y_add(0, PAIRS - 1, 2 * PAIRS - 2)
            y_add(1, PAIRS - 1, 2 * PAIRS - 1)
            y_add(0, PAIRS, 2 * PAIRS)

            dve.wait_ge(s.shared_in, 64)

            def add_up(p, h, g):
                dve.wait_ge(sum_done[p], h + 1)
                dve.wait_ge(out_stored[p], 16 * h)
                dve.tensor_tensor(total[:, p, :, :], bank[4 + p][:, :].rearrange("p (b d) -> p b d", b=GB),
                                  projs_b[:, :].unsqueeze(1).broadcast_to([P, GB, P]), ALU.add
                                  ).then_inc(s.base_added, 1)
                dve.tensor_copy(gate_now[:, p, :, :], gate_of[:, :, bass.ds(g * GB, GB)]).then_inc(s.base_added, 1)
                dve.wait_ge(s.base_added, 4 * g + 2)
                dve.wait_ge(y_gathered[p], 128 * h + 128)
                for c in range(2):
                    for b in range(GB):
                        last = dve.scalar_tensor_tensor(total[:, p, b, :], y_in[:, p, c, b, :],
                                                        gate_now[:, p, c, b:b + 1], total[:, p, b, :],
                                                        ALU.mult, ALU.add)
                    if c == 0:
                        last.then_inc(s.base_added, 2)
                        dve.wait_ge(s.base_added, 4 * g + 4)
                last.then_inc(total_ready[p], 1)

            def group_pair(m):
                for p in range(2):
                    add_up(p, m, 2 * m + p)

            loop(dve, 0, NG // 2, group_pair)

        @block.tensor
        def _(pe):
            def mm(dst, w, rhs, start=True, stop=True):
                return pe.matmul(dst, w, rhs, start=start, stop=stop)

            pe.wait_ge(s.consts_made, CONSTS)
            pe.wait_ge(s.columns_in, 16 * 9)
            pe.transpose(bank[7][:, 0:13], vec_rows[:, :], ident[0:13, 0:13]).then_inc(s.turned_w, 1)
            pe.wait_ge(s.weights_in, 16 * 14)
            for j in range(13):
                last = pe.transpose(bank[j // 4][:, (j % 4) * P:(j % 4 + 1) * P], NAT[:, 3 + j, :], ident[:, :])
                if j % 4 == 3:
                    last.then_inc(s.turned_w, 1)
            pe.transpose(bank[3][:, P:P + E], NAT[0:E, 16, :], ident[0:E, 0:E]).then_inc(s.turned_w, 1)
            mm(bank[4][:, 0:P], NAT[:, 0, :], NAT[:, 1, :]).then_inc(s.fused_w, 1)
            pe.wait_ge(s.turned_w_out, 1)
            mm(bank[5][:, 0:3 * P], NAT[:, 2, :], WIH).then_inc(s.fused_w, 1)
            pe.wait_ge(s.weights_ready, 8)
            pe.wait_ge(s.turned_w_out, 2)
            mm(bank[6][:, 0:1], WO_T, col[:, BV:BV + 1]).then_inc(s.fused_w, 1)
            pe.wait_ge(s.weights_ready, 11)

            def slots_step(t, step, i=0):
                n = 3 * t + i
                if step == "turn":
                    pe.wait_ge(s.x2_ready, t)
                    pe.wait_ge(s.xln_ready, t + 1)
                    for b in range(GB):
                        last = pe.transpose(G3[:, b * P:(b + 1) * P], xln[:, b, :], ident[:, :])
                    last.then_inc(s.turned, 1)
                    pe.wait_ge(s.ctx_in, 16 * t + 16)
                    for b in range(GB):
                        last = pe.transpose(G0[:, b * M:(b + 1) * M], ctx_tok[:, b, :], ident[0:M, 0:M])
                    last.then_inc(s.turned, 1)
                    for b in range(GB):
                        last = pe.transpose(G2[:, b * P:(b + 1) * P], x_tok[:, b, :], ident[:, :])
                    last.then_inc(s.turned, 1)
                if step == "keys":
                    pe.wait_ge(s.ctxT_ready, t + 1)
                    mm(G1[:, 0:CM], KQ_W[:, :], ctxT[:, :]).then_inc(s.keys_done, 1)
                    for b, dst in enumerate((G0, G2, G3, G1)):
                        if b == 1:
                            pe.wait_ge(s.xT_ready, t + 1)
                        if b == 3:
                            pe.wait_ge(s.keys_ready, t + 1)
                        mm(dst[0:M, 0:3 * P], ctxT[:, b * M:(b + 1) * M], VG_W[:, :]).then_inc(s.values_done, 1)
                if step == "score":
                    pe.wait_ge(s.squared, n + 1)
                    if i == 0:
                        pe.wait_ge(s.slots_in, t + 1)
                        pe.wait_ge(s.values_by_act, 2 * t + 2)
                        pe.wait_ge(s.values_by_dve, 2 * t + 2)
                    mm(G1[0:M, :], mean_w[:, 0:M], slot_sq[:, :]).then_inc(s.sumsq_done, 1)
                    for b in range(GB):
                        last = mm(G0[0:M, b * P:(b + 1) * P], keysT[:, b * M:(b + 1) * M],
                                  slots[:, b * P:(b + 1) * P])
                    last.then_inc(s.scored, 1)
                if step == "recur":
                    mm(G2[:, :], WHH[:, 2, :], slots[:, :]).then_inc(s.hn_done, 1)
                    mm(G3[:, :], WHH[:, 0, :], slots[:, :], stop=False)
                    pe.wait_ge(s.slot_ln, n + 1)
                    mm(G1[:, :], WHH[:, 1, :], slots[:, :], stop=False)
                if step == "share_sum":
                    pe.wait_ge(s.rz_ready, n + 1)
                    for b in range(GB):
                        last = mm(G0[0:M, b * P:(b + 1) * P], prob_rz[0:M + 1, b:b + 1].broadcast_to([M + 1, M]),
                                  prob[0:M + 1, b * P:(b + 1) * P])
                    last.then_inc(s.share_summed, 1)
                if step == "gates":
                    pe.wait_ge(s.share_ready, n + 1)
                    for gate, dst, done in ((0, G3, s.r_done), (2, G0, s.xn_done), (1, G1, s.z_done)):
                        for b in range(GB):
                            last = pe.matmul(dst[:, b * P:(b + 1) * P], values[:, b, gate * P:(gate + 1) * P],
                                             share[:, b * P:(b + 1) * P], start=(gate == 2),
                                             stop=(gate == 2 or b == GB - 1))
                        last.then_inc(done, 1)
                if step == "center":
                    pe.wait_ge(s.x1_ready, t + 1)
                    mm(G0[:, :], center_w[:, :], x1[:, :]).then_inc(s.c1_done, 1)
                if step == "spread":
                    pe.wait_ge(s.c1_squared, t + 1)
                    mm(G1[:, :], mean_w[:, :], c1_sq[:, :]).then_inc(s.v1_done, 1)
                if step == "route":
                    pe.wait_ge(s.xn1_ready, t + 1)
                    for b in range(GB):
                        last = mm(G2[:, b * E:(b + 1) * E], xn1[:, b * P:(b + 1) * P], RT[:, :])
                    last.then_inc(s.logits1_done, 1)
                    mm(G3[:, :], A0_T, xn1[:, :]).then_inc(s.down_done, 1)
                    mm(G1[:, :], W0_T, xn1[:, :], stop=False)
                if step == "turn_gate":
                    pe.wait_ge(s.gate_ready, t + 1)
                    for b in range(GB):
                        last = pe.transpose(G0[:, b * P:(b + 1) * P], gate_x[:, b, :, :].rearrange("p e r -> p (e r)"),
                                            ident[:, :])
                    last.then_inc(s.gate_turned, 1)
                if step == "out":
                    pe.wait_ge(s.down_ready, t + 1)
                    mm(G1[:, :], LB_T, down[:, :], start=False).then_inc(s.ffn1_done, 1)

            def heads_step(a, step, k=0):
                n = UNITS * a + k
                if step == "keys":
                    pe.wait_ge(s.head_pT_ready, UNITS * a)
                    pe.wait_ge(s.attended, a)
                    mm(BT[:, 0:CM], WK_T, ctxT[:, :]).then_inc(s.k_done, 1)
                    for b in range(GB):
                        last = mm(BO[0:M, b * P:(b + 1) * P], ctxT[:, b * M:(b + 1) * M], WV_T)
                    last.then_inc(s.v_done, 1)
                if step == "norm":
                    pe.wait_ge(s.x2_ready, a + 1)
                    pe.wait_ge(s.v_ready, a + 1)
                    mm(BO[:, :], center_w[:, :], x2[:, :]).then_inc(s.c2_done, 1)
                if step == "norm_spread":
                    pe.wait_ge(s.c2_squared, a + 1)
                    pe.wait_ge(s.k_ready, a + 1)
                    mm(BT[:, :], mean_w[:, :], c2_sq[:, :]).then_inc(s.v2_done, 1)
                if step == "project":
                    pe.wait_ge(s.xn2_ready, a + 1)
                    pe.wait_ge(s.xn3_tok_ready, a)
                    mm(BS[:, :], WQ_T, xn2[:, :]).then_inc(s.q_done, 1)
                if step == "unit_score":
                    b, u = k // 4, k % 4
                    if k == 0:
                        pe.wait_ge(s.k_ready, a + 1)
                        pe.wait_ge(s.q_by_act, 2 * a + 2)
                        pe.wait_ge(s.q_by_dve, 2 * a + 2)
                    else:
                        pe.wait_ge(s.head_shifted, n)
                    mm(BS[:, 0:Q * M], q_mask[:, u, b * P:(b + 1) * P],
                       k_quad[:, b, :, :].rearrange("p g m -> p (g m)")).then_inc(s.head_scored, 1)
                if step == "unit_turn":
                    pe.wait_ge(s.head_exp, n + 1)
                    if k > 0:
                        pe.wait_ge(s.head_pT_ready, n)
                    for g in range(Q):
                        last = pe.transpose(BT[0:M, g * P:(g + 1) * P], head_p[:, k % 2, g, :], ident[:, :])
                    last.then_inc(s.head_turned, 1)
                if step == "unit_attend":
                    b, u = k // 4, k % 4
                    pe.wait_ge(s.head_pT_ready, n + 1)
                    if k == 0:
                        pe.wait_ge(s.scatter_ready, a)
                    for bnk, w in ((BO, None), (BZ, sum_w)):
                        for g in range(Q):
                            lhs = v_pad[:, b * Q + g, 32 * u:32 * u + 32] if w is None else sum_w[0:M, u, :]
                            last = pe.matmul(bnk[32 * g:32 * g + 32, b * P:(b + 1) * P], lhs,
                                             head_pT[:, k % 2, g * P:(g + 1) * P],
                                             start=(u == 0), stop=(u == 3))
                    last.then_inc(s.head_summed, 1)
                if step == "mix":
                    pe.wait_ge(s.attended, a + 1)
                    mm(BS[:, :], WO_T, o_all[:, :]).then_inc(s.wo_done, 1)
                if step == "center":
                    pe.wait_ge(s.x3_ready, a + 1)
                    mm(BS[:, :], center_w[:, :], x3[:, :]).then_inc(s.c3_done, 1)
                if step == "spread":
                    pe.wait_ge(s.c3_squared, a + 1)
                    mm(BZ[:, :], mean_w[:, :], c3_sq[:, :]).then_inc(s.v3_done, 1)
                if step == "route":
                    pe.wait_ge(s.xn3_ready, a + 1)
                    for b in range(GB):
                        last = mm(BZ[:, b * E:(b + 1) * E], xn3[:, b * P:(b + 1) * P], WR[:, :])
                    last.then_inc(s.logits2_done, 1)
                    for b in range(GB):
                        last = pe.transpose(BS[:, b * P:(b + 1) * P], xn3[:, b * P:(b + 1) * P], ident[:, :])
                    last.then_inc(s.xn3_turned, 1)
                if step == "rank":
                    pe.wait_ge(s.both_ready, a + 1)
                    both = mo["both"][:, :, :].rearrange("p b e -> p (b e)")
                    mm(BZ[:, GB * E:2 * GB * E], before[:, :], both)
                    mm(BZ[:, 2 * GB * E:3 * GB * E], ones[:, :], both).then_inc(s.ranks_done, 1)

            groups(pe, slots_step, heads_step)

            pe.wait_ge(s.x2_ready, NG)
            pe.wait_ge(s.scatter_ready, NG)
            pe.wait_ge(s.xn3_tok_ready, NG)

            def turn(p, h):
                pe.wait_ge(rows_in[p], 16 * h + 16)
                pe.wait_ge(rowsT_ready[p], h)
                for c in range(2):
                    last = pe.transpose(ROWS[p][:, c * P:(c + 1) * P], rows[:, p, c, :], ident[:, :])
                last.then_inc(rows_turned[p], 1)

            def fc(p, h):
                pe.wait_ge(rowsT_ready[p], h + 1)
                pe.wait_ge(fc_w_in[p], h + 1)
                pe.wait_ge(gelu_done[p], h)
                for c in range(HC):
                    last = mm(FC[p][c // 2][:, (c % 2) * ER:(c % 2 + 1) * ER], fc_w[:, p, c:HID:HC], rowsT[:, p, :])
                last.then_inc(fc_done[p], 1)

            def proj(p, h):
                pe.wait_ge(gelu_done[p], h + 1)
                pe.wait_ge(proj_w_in[p], h + 1)
                pe.wait_ge(y_ready[p], h)
                for i in range(2):
                    for c in range(HC):
                        last = mm(YP[p][:, i * P:(i + 1) * P], hidden[:, p, c, i * P:(i + 1) * P],
                                  proj_w[:, p, c * P:(c + 1) * P], start=(c == 0), stop=(c == HC - 1))
                last.then_inc(proj_done[p], 1)

            turn(0, 0)
            turn(1, 0)
            fc(0, 0)
            def tile_pair(m):
                turn(0, m)
                fc(1, m - 1)
                proj(0, m - 1)
                turn(1, m)
                fc(0, m)
                proj(1, m - 1)

            loop(pe, 1, PAIRS, tile_pair)
            turn(0, PAIRS)
            fc(1, PAIRS - 1)
            proj(0, PAIRS - 1)
            fc(0, PAIRS)
            proj(1, PAIRS - 1)
            proj(0, PAIRS)

            pe.wait_ge(s.shared_in, 64)
            for p in range(2):
                pe.wait_ge(gelu_done[p], PAIRS + 1 - p)
                pe.wait_ge(y_ready[p], PAIRS + 1 - p)

            def fc_shared(p, h, first=False):
                pe.wait_ge(c_xn3_in[p], 16 * h + 16)
                for c in range(HC):
                    if p == 1:
                        pe.wait_ge(gelu_s_done[0], HC * h + c + 1)
                    elif not first:
                        pe.wait_ge(gelu_s_done[1], HC * h - HC + c + 1)
                    mm(bank[c][:, :], fcs_w[:, c:HID:HC], xn3_in[:, p, :]).then_inc(fc_s_done[p], 1)

            def sum_shared(p, h):
                pe.wait_ge(gelu_s_done[p], HC * h + HC)
                pe.wait_ge(c_x3_in[p], 16 * h + 16)
                pe.wait_ge(total_ready[p], h)
                for b in range(GB):
                    cols = slice(b * P, (b + 1) * P)
                    mm(bank[4 + p][:, cols], x3_in[:, p, cols], ident[:, :], stop=False)
                    for c in range(HC):
                        last = mm(bank[4 + p][:, cols], hidden_s[:, p, c, cols], projs_w[:, c, :],
                                  start=False, stop=(c == HC - 1))
                last.then_inc(sum_done[p], 1)

            fc_shared(0, 0, first=True)
            fc_shared(1, 0)
            sum_shared(0, 0)
            def group_pair(m):
                fc_shared(0, m)
                sum_shared(1, m - 1)
                fc_shared(1, m)
                sum_shared(0, m)

            loop(pe, 1, NG // 2, group_pair)
            sum_shared(1, NG // 2 - 1)


_INS = ['x', 'ctx_1024', 'L0_xattn_Wq', 'L0_xattn_Wk', 'L0_xattn_Wv', 'L0_xattn_gru_wih', 'L0_xattn_gru_whh',
        'L0_xattn_gru_bih', 'L0_xattn_gru_bhh', 'L0_xattn_slot_norm_w', 'L0_xattn_input_norm_w', 'L0_ffn_W',
        'L0_ffn_b', 'L0_ffn_R', 'L0_ffn_A', 'L0_ffn_B', 'L1_xattn_Wq', 'L1_xattn_bq', 'L1_xattn_Wk', 'L1_xattn_bk',
        'L1_xattn_Wv', 'L1_xattn_bv', 'L1_xattn_Wo', 'L1_xattn_bo', 'L1_ffn_Wfc_s', 'L1_ffn_bfc_s',
        'L1_ffn_Wproj_s', 'L1_ffn_bproj_s', 'L1_ffn_Wr', 'L1_ffn_Wfc', 'L1_ffn_bfc', 'L1_ffn_Wproj', 'L1_ffn_bproj']
_OUTS = [((64, 128, 128), 'float32')]


def kernel(**inputs):
    import numpy as _np
    import concourse.bacc as _bacc
    from concourse import mybir as _mybir
    from concourse.bass_utils import run_bass_kernel_spmd as _run

    nc = _bacc.Bacc("TRN2", target_bir_lowering=False, num_devices=1)
    arrays, args = {}, []
    for name in _INS:
        a = _np.ascontiguousarray(inputs[name])
        arrays[f"in_{name}_dram"] = a
        args.append(nc.dram_tensor(f"in_{name}_dram", a.shape, _mybir.dt.from_np(a.dtype), kind="ExternalInput").ap())
    for i, (shape, dtype) in enumerate(_OUTS):
        dt = _mybir.dt.from_np(_np.dtype(dtype))
        args.append(nc.dram_tensor(f"out_{i}_dram", shape, dt, kind="ExternalOutput").ap())
    two_layers(nc, *args)
    r = _run(nc, [arrays], core_ids=[0])
    got = tuple(r.results[0][f"out_{i}_dram"] for i in range(len(_OUTS)))
    return got[0]
```
